# Optimizing a Trainium2 kernel written in Bass

```python
import numpy as np
import jax
import jax.numpy as jnp

def _softmax(x, axis=-1):
    return jax.nn.softmax(x, axis=axis)

def _gelu(x):
    return jax.nn.gelu(x, approximate=True)

def _silu(x):
    return jax.nn.silu(x)

def _sigmoid(x):
    return jax.nn.sigmoid(x)

def _layernorm(x, axis=-1, eps=1e-05):
    m = jnp.mean(x, axis=axis, keepdims=True)
    v = jnp.var(x, axis=axis, keepdims=True)
    return (x - m) / jnp.sqrt(v + eps)

def _scatter_add(tgt, idx, src, axis=0):
    return tgt.at[idx].add(src)

def _segment_sum(src, seg, n):
    return jax.ops.segment_sum(src, seg, n)
kernel_name = 'mk_prb_d1_jaxref_r8_d83dfd'

def setup_inputs(seed: int=0):
    np.random.seed(seed)
    _w = jnp.asarray

    def _L0_attn_setup():
        import jax, jax.numpy as jnp
        import numpy as np
        H = 32
        G = 8
        D = 128
        HID = 512
        THETA = 10000.0

        def _rope(x, pos):
            half = D // 2
            inv_freq = 1.0 / THETA ** (jnp.arange(0, half, dtype=jnp.float32) / half)
            ang = pos[:, None].astype(jnp.float32) * inv_freq[None, :]
            cos = jnp.cos(ang)[None, None]
            sin = jnp.sin(ang)[None, None]
            x1, x2 = (x[..., :half], x[..., half:])
            return jnp.concatenate([x1 * cos - x2 * sin, x1 * sin + x2 * cos], axis=-1)
        key = jax.random.key(seed)
        ks = jax.random.split(key, 9)
        s = 0.02
        return {'hidden_states': jax.random.normal(ks[0], (1, 256, HID), jnp.float32), 'Wq': jax.random.normal(ks[1], (HID, H * D), jnp.float32) * s, 'bq': jnp.zeros((H * D,), jnp.float32), 'Wk': jax.random.normal(ks[2], (HID, G * D), jnp.float32) * s, 'bk': jnp.zeros((G * D,), jnp.float32), 'Wv': jax.random.normal(ks[3], (HID, G * D), jnp.float32) * s, 'bv': jnp.zeros((G * D,), jnp.float32), 'Wo': jax.random.normal(ks[4], (H * D, HID), jnp.float32) * s, 'bo': jnp.zeros((HID,), jnp.float32)}
    _L0_attn_in = _L0_attn_setup()

    def _L0_ffn_setup():
        import jax, jax.numpy as jnp
        import numpy as np
        ALPHA = 32
        R = 16
        SCALING = ALPHA / R
        key = jax.random.key(seed)
        k1, k2, k3, k4 = jax.random.split(key, 4)
        B_, S, D = (4, 256, 512)
        H, r, O = (8, R, 512)
        x = jax.random.normal(k1, (B_, S, D), dtype=jnp.float32)
        A = jax.random.normal(k2, (H, r, D), dtype=jnp.float32) * 0.02
        Bm = jax.random.normal(k3, (H, O, r), dtype=jnp.float32) * 0.02
        Wr = jax.random.normal(k4, (H, D), dtype=jnp.float32) * 0.02
        br = jnp.zeros((H,), dtype=jnp.float32)
        return {'x': x, 'A': A, 'B': Bm, 'Wr': Wr, 'br': br}
    _L0_ffn_in = _L0_ffn_setup()
    _d = {'L0_attn_hidden_states': _L0_attn_in['hidden_states'], 'L0_attn_Wq': _L0_attn_in['Wq'], 'L0_attn_bq': _L0_attn_in['bq'], 'L0_attn_Wk': _L0_attn_in['Wk'], 'L0_attn_bk': _L0_attn_in['bk'], 'L0_attn_Wv': _L0_attn_in['Wv'], 'L0_attn_bv': _L0_attn_in['bv'], 'L0_attn_Wo': _L0_attn_in['Wo'], 'L0_attn_bo': _L0_attn_in['bo'], 'L0_ffn_A': _L0_ffn_in['A'], 'L0_ffn_B': _L0_ffn_in['B'], 'L0_ffn_Wr': _L0_ffn_in['Wr'], 'L0_ffn_br': _L0_ffn_in['br']}
    _x0 = _d['L0_attn_hidden_states']
    _d['L0_attn_hidden_states'] = jax.random.normal(jax.random.fold_in(jax.random.key(seed), 1), (1, 1024, 512), dtype=_x0.dtype)
    del _x0
    return _d

def reference(L0_attn_hidden_states, L0_attn_Wq, L0_attn_bq, L0_attn_Wk, L0_attn_bk, L0_attn_Wv, L0_attn_bv, L0_attn_Wo, L0_attn_bo, L0_ffn_A, L0_ffn_B, L0_ffn_Wr, L0_ffn_br):

    def _L0_attn_ref(hidden_states, Wq, bq, Wk, bk, Wv, bv, Wo, bo):
        import jax, jax.numpy as jnp
        import numpy as np
        H = 32
        G = 8
        D = 128
        HID = 512
        THETA = 10000.0

        def _rope(x, pos):
            half = D // 2
            inv_freq = 1.0 / THETA ** (jnp.arange(0, half, dtype=jnp.float32) / half)
            ang = pos[:, None].astype(jnp.float32) * inv_freq[None, :]
            cos = jnp.cos(ang)[None, None]
            sin = jnp.sin(ang)[None, None]
            x1, x2 = (x[..., :half], x[..., half:])
            return jnp.concatenate([x1 * cos - x2 * sin, x1 * sin + x2 * cos], axis=-1)
        B, S, _ = hidden_states.shape
        R = H // G
        q = hidden_states @ Wq + bq
        k = hidden_states @ Wk + bk
        v = hidden_states @ Wv + bv
        q = q.reshape(B, S, H, D).transpose(0, 2, 1, 3)
        k = k.reshape(B, S, G, D).transpose(0, 2, 1, 3)
        v = v.reshape(B, S, G, D).transpose(0, 2, 1, 3)
        pos = jnp.arange(S)
        q = _rope(q, pos)
        k = _rope(k, pos)
        qg = q.reshape(B, G, R, S, D)
        scores = jnp.einsum('bgrsd,bgtd->bgrst', qg, k) / jnp.sqrt(jnp.float32(D))
        causal = jnp.tril(jnp.ones((S, S), dtype=bool))
        scores = jnp.where(causal[None, None, None], scores, jnp.finfo(scores.dtype).min)
        probs = jax.nn.softmax(scores, axis=-1)
        ctx = jnp.einsum('bgrst,bgtd->bgrsd', probs, v)
        ctx = ctx.reshape(B, H, S, D).transpose(0, 2, 1, 3).reshape(B, S, H * D)
        return ctx @ Wo + bo

    def _L0_ffn_ref(x, A, B, Wr, br):
        import jax, jax.numpy as jnp
        import numpy as np
        ALPHA = 32
        R = 16
        SCALING = ALPHA / R
        H = A.shape[0]
        router_logits = jnp.einsum('bsd,hd->bsh', x, Wr) + br
        scores = H * jax.nn.softmax(router_logits, axis=-1)
        low = jnp.einsum('bsd,hrd->bshr', x, A)
        out = jnp.einsum('bshr,hor,bsh->bso', low, B, scores)
        return SCALING * out
    x = L0_attn_hidden_states
    xn = _layernorm(x, axis=-1)
    x = x + _L0_attn_ref(xn, L0_attn_Wq, L0_attn_bq, L0_attn_Wk, L0_attn_bk, L0_attn_Wv, L0_attn_bv, L0_attn_Wo, L0_attn_bo) + _L0_ffn_ref(xn, L0_ffn_A, L0_ffn_B, L0_ffn_Wr, L0_ffn_br)
    return x

_drawn_inputs = setup_inputs


def setup_inputs(seed=0):
    import zlib

    import numpy as np

    out = dict(_drawn_inputs(seed))
    spreads = {'L0_attn_bq': (0.0, 0.8),
     'L0_attn_bk': (0.0, 0.8),
     'L0_attn_bv': (0.0, 0.1),
     'L0_attn_bo': (0.0, 0.1),
     'L0_ffn_br': (0.0, 0.1)}
    factors = {'L0_attn_Wq': 6.127, 'L0_attn_Wk': 5.973}
    for name, (base, spread) in spreads.items():
        noise = np.random.default_rng([zlib.crc32(name.encode()), seed]).standard_normal(out[name].shape)
        drawn = base * np.exp(spread * noise) if base else spread * noise
        out[name] = jnp.asarray(drawn.astype(out[name].dtype))
    for name, factor in factors.items():
        out[name] = (out[name] * factor).astype(out[name].dtype)
    return out
```

```python
from contextlib import ExitStack

import numpy as np

import concourse.bass as bass
from concourse import mybir

F32 = mybir.dt.float32
F32R = mybir.dt.float32r
BF16 = mybir.dt.bfloat16
ALU = mybir.AluOpType
ACT = mybir.ActivationFunctionType
AX = mybir.AxisListType

P = 128
S, HID = 1024, 512
H, G, D = 32, 8, 128
R = H // G
E, RANK = 8, 16
ER = E * RANK
KT = HID // P
NT = S // P
HALF = S // 2
BLOCKS = NT * (NT + 1) // 2
EPS = 1e-5
SCALE = float(D) ** -0.5
FFN_SCALE = 2.0 * E
MASKED = -1e30
UNITS = 2 + R
K_UNIT, V_UNIT, Q_UNIT = 0, 1, 2
PAIR = 2
PASSES = G // PAIR
STEPS = PAIR * NT
PT_SLOTS = 3
PRE_TURNS = NT + 1

SCORE_JOB = {0: (1, K_UNIT), 1: (1, Q_UNIT), 2: (1, Q_UNIT + 1), 3: (1, Q_UNIT + 3),
             4: (0, K_UNIT), 5: (0, Q_UNIT), 6: (0, Q_UNIT + 1), 7: (0, Q_UNIT + 3)}
ATTEND_JOB = {0: (1, V_UNIT), 2: (1, Q_UNIT + 2), 4: (0, V_UNIT), 6: (0, Q_UNIT + 2)}
V_TURN_STEPS = (1, 5)
SPLIT_UNITS = {1: (0, 1), 2: (2, 3), 3: (4, 5)}
SPLIT_WO = {4: 0, 5: 1, 6: 2, 7: 3}


def job_of(table, ls):
    gl, i = divmod(ls, NT)
    if i not in table:
        return None
    c, unit = table[i]
    return gl + (c == 0), c, unit


def job_index(it, gl, c, unit):
    return it * (2 * UNITS * PAIR) + 2 * UNITS * gl + UNITS * c + unit


def rope_index(it, gl, c, unit):
    return it * (2 * (UNITS - 1) * PAIR) + 2 * (UNITS - 1) * gl + (UNITS - 1) * c + max(0, unit - 1)


def v_index(it, gl, c):
    return it * (2 * PAIR) + 2 * gl + c


def turn_local(ls, t, final):
    gl, i = divmod(ls, NT)
    in_final = final and gl == PAIR - 1
    return gl * (BLOCKS + 2) + i * (i + 1) // 2 + t + (i >= 1) + (i >= 5 and not in_final)


def block_local(ls, t):
    gl, i = divmod(ls, NT)
    return gl * BLOCKS + i * (i + 1) // 2 + t


def half_slot(gl, c):
    return 2 if c else gl % 2


def build(nc, x, wq, wk, wv, wo, biases, bo, cos_t, sin_t, aw, b_t, br, out):
    x_v = x.rearrange("a (n p) d -> p (a n) d", p=P)
    out_v = out.rearrange("a (n p) d -> p (a n) d", p=P)
    w_v = {K_UNIT: wk.rearrange("(k p) n -> p k n", p=P),
           V_UNIT: wv.rearrange("(k p) n -> p k n", p=P),
           Q_UNIT: wq.rearrange("(k p) n -> p k n", p=P)}
    aw_v = aw.rearrange("(k p) n -> p k n", p=P)

    with ExitStack() as ctx:
        def sb(name, shape, dt=F32):
            return ctx.enter_context(nc.sbuf_tensor(name, shape, dt))

        def ps(name, shape):
            return ctx.enter_context(nc.psum_tensor(name, shape, F32))

        def sem(name):
            return ctx.enter_context(nc.semaphore(name))

        xT_hi = sb("xT_hi", [P, KT, S], F32R)
        xT_lo = sb("xT_lo", [P, KT, S], F32R)
        kT_hi = sb("kT_hi", [P, 3, HALF], F32R)
        kT_lo = sb("kT_lo", [P, 3, HALF], F32R)
        v_hi = sb("v_hi", [P, 3, HALF // P, D], F32R)
        v_lo = sb("v_lo", [P, 3, HALF // P, D], F32R)
        qT_hi = sb("qT_hi", [P, R, S], F32R)
        qT_lo = sb("qT_lo", [P, R, S], F32R)
        w_hi = sb("w_hi", [P, UNITS, KT, D], F32R)
        w_lo = sb("w_lo", [P, UNITS, KT, D], F32R)
        wo_hi = sb("wo_hi", [P, 2, R, HID], F32R)
        wo_lo = sb("wo_lo", [P, 2, R, HID], F32R)
        w_stage = sb("w_stage", [P, 2, KT, D])
        wo_stage = sb("wo_stage", [P, 2, HID])
        cos_sb = sb("cos_sb", [P, S])
        sin_sb = sb("sin_sb", [P, S])
        acc = sb("acc", [P, NT, HID])
        probs = sb("probs", [P, R, S])
        pT_hi = sb("pT_hi", [P, PT_SLOTS, R * P], F32R)
        pT_lo = sb("pT_lo", [P, PT_SLOTS, R * P], F32R)
        rot = sb("rot", [P, 2, HALF])
        straight = sb("straight", [P, 2, HALF])
        vT = sb("vT", [P, HALF])
        ctx_hi = sb("ctx_hi", [P, R * P], F32R)
        ctx_lo = sb("ctx_lo", [P, R * P], F32R)
        bias_all = sb("bias_all", [P, G, UNITS])
        bias_now = sb("bias_now", [P, 2, UNITS])
        ident = sb("ident", [P, P])
        ident_b = sb("ident_b", [P, P], BF16)
        mask_b = sb("mask_b", [P, P], BF16)
        neg_max = sb("neg_max", [P, R])
        exp_bias = sb("exp_bias", [P, R])
        row_sum = sb("row_sum", [P, R])
        row_inv = sb("row_inv", [P, R])
        stats = sb("stats", [P, NT, 6])
        mean_var = sb("mean_var", [P, NT, 2])
        std = sb("std", [P, NT])
        rstd = sb("rstd", [P, NT])
        logits = sb("logits", [P, NT, E])
        br_sb = sb("br_sb", [P, E])
        gate_neg = sb("gate_neg", [P, NT])
        gate_sum = sb("gate_sum", [P, NT])
        gate_inv = sb("gate_inv", [P, NT])
        xn = probs[:, 0, :].rearrange("p (b d) -> p b d", b=2)
        xT_f = probs[:, 1, :].rearrange("p (b k t) -> p b k t", b=2, k=KT)
        aw_sb = probs[:, 2, 0:KT * (ER + E)].rearrange("p (k n) -> p k n", k=KT)
        lowT = probs[:, 2, KT * (ER + E):KT * (ER + E) + 2 * P].rearrange("p (b t) -> p b t", b=2)
        bt_sb = probs[:, 3, 0:HID]
        bo_sb = probs[:, 3, HID:2 * HID]
        low = wo_stage[:, :, :].rearrange("p b (n e) -> p (b n) e", e=ER)

        score_ps = [ps("score0", [P, S]), ps("score1", [P, S])]
        turn_ps = [ps("turn0", [P, HID]), ps("turn1", [P, HID])]
        ctx_ps = ps("ctx", [P, HID])
        proj_ps = ps("proj", [P, HALF])

        x_loaded = [sem("x_loaded0"), sem("x_loaded1")]
        aw_loaded, bias_loaded, br_loaded = sem("aw_loaded"), sem("bias_loaded"), sem("br_loaded")
        cos_loaded, sin_loaded = sem("cos_loaded"), sem("sin_loaded")
        bt_loaded, bo_loaded = sem("bt_loaded"), sem("bo_loaded")
        w_loaded = [sem("w_loaded0"), sem("w_loaded1")]
        wo_loaded = [sem("wo_loaded0"), sem("wo_loaded1")]
        out_stored = sem("out_stored")
        turned = sem("turned")
        scored = sem("scored")
        projected = sem("projected")
        block_summed = sem("block_summed")
        out_projected = sem("out_projected")
        gated_in = sem("gated_in")
        low_turned = sem("low_turned")
        ffn_out = sem("ffn_out")
        turn_hi = sem("turn_hi")
        exps = sem("exps")
        v_taken = sem("v_taken")
        swapped = sem("swapped")
        ctx_hi_done = sem("ctx_hi_done")
        std_done = sem("std_done")
        xT_f_done = sem("xT_f_done")
        gate_exp = sem("gate_exp")
        lowT_done = sem("lowT_done")
        turn_lo = sem("turn_lo")
        max_done = sem("max_done")
        bias_done = sem("bias_done")
        inv_done = sem("inv_done")
        probs_done = sem("probs_done")
        cos_done = sem("cos_done")
        ctx_lo_done = sem("ctx_lo_done")
        acc_added = sem("acc_added")
        ln_step = sem("ln_step")
        xn_done = sem("xn_done")
        low_read = sem("low_read")
        gate_step = sem("gate_step")
        const_step = sem("const_step")
        consts_done = sem("consts_done")
        w_hi_done, w_split = sem("w_hi_done"), sem("w_split")
        wo_hi_done, wo_split = sem("wo_hi_done"), sem("wo_split")
        biases_set = sem("biases_set")
        bo_added = sem("bo_added")
        sin_done, rope_summed, rope_hi = sem("sin_done"), sem("rope_summed"), sem("rope_hi")
        roped = sem("roped")

        block = ctx.enter_context(nc.Block())

        def split_dst(gl, c, unit):
            if unit == K_UNIT:
                return kT_hi[:, half_slot(gl, c), :], kT_lo[:, half_slot(gl, c), :]
            h = unit - Q_UNIT
            return qT_hi[:, h, c * HALF:(c + 1) * HALF], qT_lo[:, h, c * HALF:(c + 1) * HALF]

        @block.sync
        def _(sp):
            def load_unit(g, u):
                view = w_v[min(u, Q_UNIT)]
                col = g * (R * D) + (u - Q_UNIT) * D if u >= Q_UNIT else g * D
                sp.dma_start(w_stage[:, u % 2], view[:, :, bass.ds(col, D)]).then_inc(w_loaded[u % 2], 16)

            def load_wo(g, h):
                sp.dma_start(wo_stage[:, h % 2, :], wo[bass.ds(g * (R * D) + h * D, D), :])\
                    .then_inc(wo_loaded[h % 2], 16)

            for c in range(2):
                sp.dma_start(acc[:, c * NT // 2:(c + 1) * NT // 2, :],
                             x_v[:, c * NT // 2:(c + 1) * NT // 2, :]).then_inc(x_loaded[c], 16)
            for u in range(UNITS):
                if u >= 2:
                    sp.wait_ge(w_split, u - 1)
                load_unit(0, u)
            for h in range(R):
                if h < 2:
                    sp.wait_ge(low_turned, NT)
                else:
                    sp.wait_ge(wo_split, h - 1)
                load_wo(0, h)

            def one_pass(it, final):
                for gl in range(PAIR):
                    if final and gl == PAIR - 1:
                        break
                    for u in range(UNITS):
                        sp.wait_ge(w_split, it * (UNITS * PAIR) + UNITS * (gl + 1) + u - 1)
                        load_unit(it * PAIR + gl + 1, u)
                    for h in range(R):
                        sp.wait_ge(wo_split, it * (R * PAIR) + R * (gl + 1) + h - 1)
                        load_wo(it * PAIR + gl + 1, h)

            with sp.Fori(0, PASSES - 1) as it:
                one_pass(it, False)
            one_pass(PASSES - 1, True)
            for i in range(NT):
                sp.wait_ge(acc_added, NT + (G - 1) * NT + i + 1)
                sp.dma_start(out_v[:, i, :], acc[:, i, :]).then_inc(out_stored, 16)
            sp.wait_ge(out_stored, 16 * NT)

        @block.gpsimd
        def _(pool):
            def split_unit(it, gl, u):
                n = it * (UNITS * PAIR) + UNITS * gl + u
                pool.wait_ge(w_hi_done, n + 1)
                pool.tensor_tensor(w_lo[:, u], w_stage[:, u % 2], w_hi[:, u].bitcast(F32),
                                   ALU.subtract).then_inc(w_split, 1)

            def split_wo(it, gl, h):
                n = it * (R * PAIR) + R * gl + h
                pool.wait_ge(wo_hi_done, n + 1)
                pool.tensor_tensor(wo_lo[:, gl % 2, h, :], wo_stage[:, h % 2, :],
                                   wo_hi[:, gl % 2, h, :].bitcast(F32), ALU.subtract).then_inc(wo_split, 1)

            def rope(it, gl, c, unit):
                n = rope_index(it, gl, c, unit)
                b = rope_index(0, gl, c, unit) % 2
                hi, lo = split_dst(gl, c, unit)
                pool.wait_ge(swapped, (n + 1) * 2)
                pool.tensor_tensor(rot[:, b], rot[:, b], sin_sb[:, c * HALF:(c + 1) * HALF],
                                   ALU.mult).then_inc(sin_done, 1)
                pool.wait_ge(sin_done, n + 1)
                pool.wait_ge(cos_done, n + 1)
                pool.tensor_tensor(hi, straight[:, b], rot[:, b], ALU.add).then_inc(rope_hi, 1)
                pool.wait_ge(rope_hi, n + 1)
                pool.tensor_tensor(straight[:, b], straight[:, b], rot[:, b], ALU.add).then_inc(rope_summed, 1)
                pool.wait_ge(rope_summed, n + 1)
                pool.tensor_tensor(lo, straight[:, b], hi.bitcast(F32), ALU.subtract).then_inc(roped, 1)

            def set_biases(g, slot):
                pool.tensor_copy(bias_now[:, slot:slot + 1, :], bias_all[:, bass.ds(g, 1), :]).then_inc(biases_set, 1)

            pool.memset(ident[:], 0.0).then_inc(const_step, 1)
            pool.memset(ident_b[:], 0.0).then_inc(const_step, 1)
            pool.memset(mask_b[:], 0.0).then_inc(const_step, 1)
            pool.wait_ge(const_step, 3)
            for tile in (ident, ident_b):
                pool.affine_select(out=tile[:], in_=tile[:], compare_op=ALU.not_equal, fill=1.0, base=0,
                                   pattern=[[-1, P]], channel_multiplier=1).then_inc(consts_done, 1)
            pool.affine_select(out=mask_b[:], in_=mask_b[:], compare_op=ALU.is_ge, fill=MASKED, base=0,
                               pattern=[[-1, P]], channel_multiplier=1).then_inc(consts_done, 1)
            pool.wait_ge(bias_loaded, 16)
            set_biases(0, 0)
            for u in range(4):
                split_unit(0, 0, u)
            pool.wait_ge(bo_loaded, 16)

            def add_bo(n):
                pool.wait_ge(xn_done, n + 1)
                pool.tensor_tensor(acc[:, n, :], acc[:, n, :], bo_sb, ALU.add).then_inc(bo_added, 1)

            for n in range(4):
                add_bo(n)
            for u in range(4, UNITS):
                split_unit(0, 0, u)
            for n in range(4, NT):
                add_bo(n)
            pool.wait_ge(sin_loaded, 16)
            for u in (K_UNIT, *range(Q_UNIT, UNITS)):
                rope(0, 0, 0, u)
            rope(0, *job_of(SCORE_JOB, 0))
            for h in range(R):
                split_wo(0, 0, h)

            def one_pass(it, final):
                for ls in range(STEPS):
                    gl, i = divmod(ls, NT)
                    in_final = final and gl == PAIR - 1
                    job = job_of(ATTEND_JOB, ls)
                    if job and job[2] != V_UNIT and not (in_final and job[1] == 0):
                        rope(it, *job)
                    if not in_final:
                        for u in SPLIT_UNITS.get(i, ()):
                            split_unit(it, gl + 1, u)
                        if i == 1:
                            set_biases(it * PAIR + gl + 1, (gl + 1) % 2)
                        if i in SPLIT_WO:
                            split_wo(it, gl + 1, SPLIT_WO[i])
                    if final and ls == STEPS - 1:
                        break
                    job = job_of(SCORE_JOB, ls + 1)
                    if not (final and job[0] >= PAIR):
                        rope(it, *job)

            with pool.Fori(0, PASSES - 1) as it:
                one_pass(it, False)
            one_pass(PASSES - 1, True)

        @block.scalar
        def _(act):
            def take_job(it, gl, c, unit):
                act.wait_ge(projected, job_index(it, gl, c, unit) + 1)
                bias = bias_now[:, gl % 2, unit:unit + 1]
                if unit == V_UNIT:
                    act.activation(vT[:, :], proj_ps[:, :], ACT.Identity, bias=bias).then_inc(v_taken, 1)
                    return
                n = rope_index(it, gl, c, unit)
                b = rope_index(0, gl, c, unit) % 2
                if not (isinstance(n, int) and n < 2):
                    act.wait_ge(rope_summed, n - 1)
                m = D // 2
                act.activation(rot[0:m, b, :], proj_ps[m:D, :], ACT.Identity, bias=bias[m:D]).then_inc(swapped, 1)
                act.activation(rot[m:D, b, :], proj_ps[0:m, :], ACT.Identity, bias=bias[0:m]).then_inc(swapped, 1)

            def exp_head(it, ls, h):
                n = it * (STEPS * R) + ls * R + h
                w = (ls % NT + 1) * P
                act.wait_ge(bias_done, n + 1)
                act.activation(probs[:, h, 0:w], score_ps[h % 2][:, 0:w], ACT.Exp, bias=exp_bias[:, h:h + 1],
                               scale=SCALE, accum_out=row_sum[:, h:h + 1]).then_inc(exps, 1)

            def v_turn_hi(it, ls, final):
                u = turn_local(ls, 0, final) - 1
                gl, i = divmod(ls, NT)
                slot = half_slot(gl + (i == 5), i == 1)
                act.wait_ge(turned, it * (PAIR * (BLOCKS + 2)) + PRE_TURNS + u + 1)
                act.activation(v_hi[:, slot].rearrange("p b d -> p (b d)"), turn_ps[(PRE_TURNS + u) % 2][:, :],
                               ACT.Copy).then_inc(turn_hi, 1)

            act.dma_start(aw_sb, aw_v).then_inc(aw_loaded, 16)
            act.dma_start(bias_all[:], biases).then_inc(bias_loaded, 16)
            act.dma_start(br_sb[:], br.partition_broadcast(P)).then_inc(br_loaded, 16)
            act.dma_start(cos_sb[:], cos_t).then_inc(cos_loaded, 16)
            act.dma_start(sin_sb[:], sin_t).then_inc(sin_loaded, 16)
            act.dma_start(bo_sb, bo.partition_broadcast(P)).then_inc(bo_loaded, 16)
            act.dma_start(bt_sb, b_t).then_inc(bt_loaded, 16)

            act.wait_ge(ln_step, 2)
            act.activation(std[:], std[:], ACT.Sqrt).then_inc(std_done, 1)
            for n in range(NT):
                act.wait_ge(turned, n + 1)
                if n >= 2:
                    act.wait_ge(gated_in, n - 1)
                src = turn_ps[n % 2][:, :].rearrange("p (k t) -> p k t", k=KT)
                act.activation(xT_f[:, n % 2], src, ACT.Copy).then_inc(xT_f_done, 1)
                act.activation(xT_hi[:, :, n * P:(n + 1) * P], src, ACT.Copy).then_inc(turn_hi, 1)
            act.wait_ge(gate_step, 3)
            act.activation(logits[:], logits[:], ACT.Exp).then_inc(gate_exp, 1)

            def take_lowT(n):
                act.wait_ge(low_turned, n + 1)
                if n >= 2:
                    act.wait_ge(ffn_out, n - 1)
                act.activation(lowT[:, n % 2], score_ps[n % 2][:, HID:HID + P], ACT.Copy).then_inc(lowT_done, 1)

            act.wait_ge(biases_set, 1)
            for u in range(UNITS):
                take_job(0, 0, 0, u)
                take_lowT(u)
            act.wait_ge(turned, NT + 1)
            act.activation(v_hi[:, 0].rearrange("p b d -> p (b d)"), turn_ps[NT % 2][:, :],
                           ACT.Copy).then_inc(turn_hi, 1)
            for n in range(UNITS, NT):
                take_lowT(n)
            exp_head(0, 0, 0)
            exp_head(0, 0, 1)
            take_job(0, *job_of(SCORE_JOB, 0))
            exp_head(0, 0, 2)
            exp_head(0, 0, 3)

            def one_pass(it, final):
                for ls in range(STEPS):
                    gl, i = divmod(ls, NT)
                    in_final = final and gl == PAIR - 1
                    if i in V_TURN_STEPS and not (in_final and i == 5):
                        v_turn_hi(it, ls, final)
                    for t in range(i + 1):
                        u, p = turn_local(ls, t, final), block_local(ls, t)
                        act.wait_ge(turned, it * (PAIR * (BLOCKS + 2)) + PRE_TURNS + u + 1)
                        act.wait_ge(block_summed, it * (PAIR * BLOCKS) + p + 1)
                        act.activation(pT_hi[:, p % PT_SLOTS, :], turn_ps[(PRE_TURNS + u) % 2][:, :],
                                       ACT.Copy).then_inc(turn_hi, 1)
                        if t == min(i, 1):
                            job = job_of(ATTEND_JOB, ls)
                            if job and not (in_final and job[1] == 0):
                                if job[2] == V_UNIT:
                                    act.wait_ge(biases_set, it * PAIR + job[0] + 1)
                                take_job(it, *job)
                    act.wait_ge(block_summed, it * (PAIR * BLOCKS) + block_local(ls, i) + 1 + PT_SLOTS)
                    act.activation(ctx_hi[:], ctx_ps[:, :], ACT.Copy).then_inc(ctx_hi_done, 1)
                    if final and ls == STEPS - 1:
                        break
                    exp_head(it, ls + 1, 0)
                    exp_head(it, ls + 1, 1)
                    job = job_of(SCORE_JOB, ls + 1)
                    if not (final and job[0] >= PAIR):
                        if job[2] == K_UNIT:
                            act.wait_ge(biases_set, it * PAIR + job[0] + 1)
                        take_job(it, *job)
                    exp_head(it, ls + 1, 2)
                    exp_head(it, ls + 1, 3)

            with act.Fori(0, PASSES - 1) as it:
                one_pass(it, False)
            one_pass(PASSES - 1, True)

        @block.vector
        def _(dve):
            def lo_part(out_lo, src_ps, hi):
                return dve.tensor_tensor(out_lo, src_ps, hi.bitcast(F32), ALU.subtract)

            def times_cos(it, gl, c, unit):
                n = rope_index(it, gl, c, unit)
                b = rope_index(0, gl, c, unit) % 2
                dve.wait_ge(swapped, (n + 1) * 2)
                if not (isinstance(n, int) and n < 2):
                    dve.wait_ge(roped, n - 1)
                dve.scalar_tensor_tensor(straight[:, b], proj_ps[:, :], bias_now[:, gl % 2, unit:unit + 1],
                                         cos_sb[:, c * HALF:(c + 1) * HALF], ALU.add, ALU.mult)\
                    .then_inc(cos_done, 1)

            def row_max(it, ls, h):
                n = it * (STEPS * R) + ls * R + h
                w = (ls % NT + 1) * P
                dve.wait_ge(scored, n + 1)
                dve.tensor_reduce(neg_max[:, h:h + 1], score_ps[h % 2][:, 0:w], AX.X, ALU.max).then_inc(max_done, 1)
                dve.wait_ge(max_done, n + 1)
                dve.tensor_scalar(exp_bias[:, h:h + 1], neg_max[:, h:h + 1], -SCALE, None, ALU.mult)\
                    .then_inc(bias_done, 1)

            def normalise(it, ls, h):
                n = it * (STEPS * R) + ls * R + h
                w = (ls % NT + 1) * P
                dve.wait_ge(exps, n + 1)
                dve.reciprocal(row_inv[:, h:h + 1], row_sum[:, h:h + 1]).then_inc(inv_done, 1)
                dve.wait_ge(inv_done, n + 1)
                dve.tensor_scalar(probs[:, h, 0:w], probs[:, h, 0:w], row_inv[:, h:h + 1], None, ALU.mult)\
                    .then_inc(probs_done, 1)

            def score_part(it, ls, job):
                row_max(it, ls, 0)
                row_max(it, ls, 1)
                normalise(it, ls, 0)
                normalise(it, ls, 1)
                if job:
                    times_cos(it, *job)
                row_max(it, ls, 2)
                row_max(it, ls, 3)
                normalise(it, ls, 2)
                normalise(it, ls, 3)

            def unit_hi(it, gl, u):
                dve.wait_ge(w_loaded[u % 2], (it * (UNITS * PAIR // 2) + UNITS // 2 * gl + u // 2 + 1) * 16)
                dve.tensor_copy(w_hi[:, u], w_stage[:, u % 2]).then_inc(w_hi_done, 1)

            def rows_hi(it, gl, h):
                dve.wait_ge(wo_loaded[h % 2], (it * (R * PAIR // 2) + R // 2 * gl + h // 2 + 1) * 16)
                dve.tensor_copy(wo_hi[:, gl % 2, h, :], wo_stage[:, h % 2, :]).then_inc(wo_hi_done, 1)

            for n in range(NT):
                if n % (NT // 2) == 0:
                    dve.wait_ge(x_loaded[n // (NT // 2)], 16)
                dve.bn_stats(stats[:, n, :], acc[:, n, :]).then_inc(low_read, 1)
            for n in range(NT):
                dve.wait_ge(low_read, n + 1)
                last = dve.bn_aggr(mean_var[:, n, :], stats[:, n, :])
                if n == NT - 1:
                    last.then_inc(ln_step, 1)
            dve.wait_ge(ln_step, 1)
            dve.tensor_scalar(std[:], mean_var[:, :, 1], EPS, None, ALU.add).then_inc(ln_step, 1)
            dve.wait_ge(std_done, 1)
            dve.reciprocal(rstd[:], std[:]).then_inc(ln_step, 1)
            dve.wait_ge(ln_step, 3)

            def normal_x(n):
                if n >= 2:
                    dve.wait_ge(turned, n - 1)
                dve.tensor_scalar(xn[:, n % 2], acc[:, n, :], mean_var[:, n, 0:1], rstd[:, n:n + 1],
                                  ALU.subtract, ALU.mult).then_inc(xn_done, 1)

            normal_x(0)
            for n in range(NT):
                if n + 1 < NT:
                    normal_x(n + 1)
                dve.wait_ge(turn_hi, n + 1)
                lo_part(xT_lo[:, :, n * P:(n + 1) * P],
                        turn_ps[n % 2][:, :].rearrange("p (k t) -> p k t", k=KT),
                        xT_hi[:, :, n * P:(n + 1) * P]).then_inc(turn_lo, 1)
                dve.wait_ge(gated_in, n + 1)
                dve.tensor_copy(logits[:, n, :], score_ps[n % 2][:, ER:ER + E]).then_inc(low_read, 1)
                dve.tensor_copy(low[:, n, :], score_ps[n % 2][:, 0:ER]).then_inc(low_read, 1)
                if n < UNITS:
                    unit_hi(0, 0, n)
            dve.wait_ge(low_read, 3 * NT)
            dve.wait_ge(br_loaded, 16)
            dve.tensor_tensor(logits[:], logits[:], br_sb[:, None, :].to_broadcast([P, NT, E]), ALU.add)\
                .then_inc(gate_step, 1)
            dve.wait_ge(gate_step, 1)
            dve.tensor_reduce(gate_neg[:], logits[:], AX.X, ALU.max).then_inc(gate_step, 1)
            dve.wait_ge(gate_step, 2)
            dve.tensor_tensor(logits[:], logits[:], gate_neg[:, :, None].to_broadcast([P, NT, E]), ALU.subtract)\
                .then_inc(gate_step, 1)
            dve.wait_ge(gate_exp, 1)
            dve.tensor_reduce(gate_sum[:], logits[:], AX.X, ALU.add).then_inc(gate_step, 1)
            dve.wait_ge(gate_step, 4)
            dve.reciprocal(gate_inv[:], gate_sum[:]).then_inc(gate_step, 1)
            dve.wait_ge(gate_step, 5)
            dve.tensor_scalar(gate_inv[:], gate_inv[:], FFN_SCALE, None, ALU.mult).then_inc(gate_step, 1)
            dve.wait_ge(gate_step, 6)
            dve.tensor_tensor(logits[:], logits[:], gate_inv[:, :, None].to_broadcast([P, NT, E]), ALU.mult)\
                .then_inc(gate_step, 1)
            dve.wait_ge(gate_step, 7)
            low_e = low.rearrange("p n (e r) -> p (n e) r", e=E)
            dve.tensor_tensor(low_e, low_e,
                              logits[:].rearrange("p n e -> p (n e)")[:, :, None].to_broadcast([P, NT * E, RANK]),
                              ALU.mult).then_inc(gate_step, 1)

            def add_ffn(n):
                dve.wait_ge(ffn_out, n + 1)
                dve.wait_ge(bo_added, n + 1)
                dve.tensor_tensor(acc[:, n, :], ctx_ps[:, :], acc[:, n, :], ALU.add).then_inc(acc_added, 1)

            dve.wait_ge(cos_loaded, 16)
            dve.wait_ge(biases_set, 1)
            for u in range(UNITS):
                if u != V_UNIT:
                    times_cos(0, 0, 0, u)
                if u >= 1:
                    add_ffn(u - 1)
            dve.wait_ge(turn_hi, NT + 1)
            lo_part(v_lo[:, 0].rearrange("p b d -> p (b d)"), turn_ps[NT % 2][:, :],
                    v_hi[:, 0].rearrange("p b d -> p (b d)")).then_inc(turn_lo, 1)
            for n in range(UNITS - 1, NT):
                add_ffn(n)
            score_part(0, 0, job_of(SCORE_JOB, 0))
            for h in range(R):
                rows_hi(0, 0, h)

            def one_pass(it, final):
                for ls in range(STEPS):
                    gl, i = divmod(ls, NT)
                    in_final = final and gl == PAIR - 1
                    if not in_final:
                        for u in SPLIT_UNITS.get(i, ()):
                            dve.wait_ge(projected, job_index(it, gl, 1, u) + 1)
                            unit_hi(it, gl + 1, u)
                        if i in SPLIT_WO:
                            dve.wait_ge(out_projected, it * STEPS + ls)
                            rows_hi(it, gl + 1, SPLIT_WO[i])
                    if i in V_TURN_STEPS and not (in_final and i == 5):
                        u = turn_local(ls, 0, final) - 1
                        slot = half_slot(gl + (i == 5), i == 1)
                        dve.wait_ge(turn_hi, it * (PAIR * (BLOCKS + 2)) + PRE_TURNS + u + 1)
                        lo_part(v_lo[:, slot].rearrange("p b d -> p (b d)"), turn_ps[(PRE_TURNS + u) % 2][:, :],
                                v_hi[:, slot].rearrange("p b d -> p (b d)")).then_inc(turn_lo, 1)
                    for t in range(i + 1):
                        u, p = turn_local(ls, t, final), block_local(ls, t)
                        dve.wait_ge(turn_hi, it * (PAIR * (BLOCKS + 2)) + PRE_TURNS + u + 1)
                        lo_part(pT_lo[:, p % PT_SLOTS, :], turn_ps[(PRE_TURNS + u) % 2][:, :],
                                pT_hi[:, p % PT_SLOTS, :]).then_inc(turn_lo, 1)
                        if t == min(i, 1):
                            job = job_of(ATTEND_JOB, ls)
                            if job and job[2] != V_UNIT and not (in_final and job[1] == 0):
                                times_cos(it, *job)
                    dve.wait_ge(ctx_hi_done, it * STEPS + ls + 1)
                    lo_part(ctx_lo[:], ctx_ps[:, :], ctx_hi[:]).then_inc(ctx_lo_done, 1)
                    if not (final and ls == STEPS - 1):
                        job = job_of(SCORE_JOB, ls + 1)
                        score_part(it, ls + 1, None if final and job[0] >= PAIR else job)
                    dve.wait_ge(out_projected, it * STEPS + ls + 1)
                    dve.tensor_tensor(acc[:, i, :], ctx_ps[:, :], acc[:, i, :], ALU.add).then_inc(acc_added, 1)

            with dve.Fori(0, PASSES - 1) as it:
                one_pass(it, False)
            one_pass(PASSES - 1, True)

        @block.tensor
        def _(pe):
            def three(out, pairs):
                n = len(pairs)
                for j, (a_hi, a_lo, b_hi, b_lo) in enumerate(pairs):
                    pe.matmul(out, a_hi, b_hi, start=(j == 0), stop=False)
                    pe.matmul(out, a_hi, b_lo, start=False, stop=False)
                    last = pe.matmul(out, a_lo, b_hi, start=False, stop=(j == n - 1))
                return last

            def project(it, gl, c, unit):
                if unit == V_UNIT + 1:
                    pe.wait_ge(v_taken, v_index(it, gl, c) + 1)
                elif not (isinstance(it, int) and it == 0 and gl == 0 and c == 0 and unit == 0):
                    pe.wait_ge(cos_done, rope_index(it, gl, c, unit) + (unit == V_UNIT))
                if c == 0:
                    pe.wait_ge(w_split, it * (UNITS * PAIR) + UNITS * gl + unit + 1)
                cols = slice(c * HALF, (c + 1) * HALF)
                three(proj_ps[:, :], [(w_hi[:, unit, k, :], w_lo[:, unit, k, :], xT_hi[:, k, cols], xT_lo[:, k, cols])
                                      for k in range(KT)]).then_inc(projected, 1)

            def score(it, ls, h):
                gl, i = divmod(ls, NT)
                n = it * (STEPS * R) + ls * R + h
                if not (isinstance(n, int) and n < 2):
                    pe.wait_ge(exps, n - 1)
                if i % (NT // 2) == 0:
                    pe.wait_ge(roped, rope_index(it, gl, i // (NT // 2), Q_UNIT + h) + 1)
                w = (i + 1) * P
                q_hi, q_lo = qT_hi[:, h, i * P:(i + 1) * P], qT_lo[:, h, i * P:(i + 1) * P]
                for c in range(2 if w > HALF else 1):
                    m = max(2 * P, min(HALF, w - c * HALF))
                    o = score_ps[h % 2][:, c * HALF:c * HALF + m]
                    slot = half_slot(gl, c)
                    diagonal = w - c * HALF <= HALF
                    pe.matmul(o, q_hi, kT_hi[:, slot, 0:m], start=True, stop=False)
                    pe.matmul(o, q_hi, kT_lo[:, slot, 0:m], start=False, stop=False)
                    last = pe.matmul(o, q_lo, kT_hi[:, slot, 0:m], start=False, stop=not diagonal)
                last = pe.matmul(score_ps[h % 2][:, w - P:w], ident_b[:], mask_b[:], start=False, stop=True)
                last.then_inc(scored, 1)

            def turn_v(u):
                for b in range(HALF // P):
                    last = pe.transpose(turn_ps[u % 2][:, b * P:(b + 1) * P], vT[:, b * P:(b + 1) * P], ident[:])
                last.then_inc(turned, 1)

            pe.wait_ge(consts_done, 3)
            pe.wait_ge(aw_loaded, 16)

            def gate_in(n):
                pe.wait_ge(xT_f_done, n + 1)
                if n >= 2:
                    pe.wait_ge(low_read, NT + 2 * (n - 1))
                for k in range(KT):
                    last = pe.matmul(score_ps[n % 2][:, 0:ER + E], xT_f[:, n % 2, k, :], aw_sb[:, k, :],
                                     start=(k == 0), stop=(k == KT - 1))
                last.then_inc(gated_in, 1)

            for n in range(NT):
                pe.wait_ge(xn_done, n + 1)
                if n >= 2:
                    pe.wait_ge(turn_lo, n - 1)
                for k in range(KT):
                    last = pe.transpose(turn_ps[n % 2][:, k * P:(k + 1) * P], xn[:, n % 2, k * P:(k + 1) * P],
                                        ident[:])
                    if n == 0 and k < PT_SLOTS:
                        last.then_inc(block_summed, 1)
                last.then_inc(turned, 1)
                if n >= 1:
                    gate_in(n - 1)
            gate_in(NT - 1)

            def turn_low(n):
                if n == 0:
                    pe.wait_ge(gate_step, 8)
                if n >= 2:
                    pe.wait_ge(lowT_done, n - 1)
                pe.transpose(score_ps[n % 2][:, HID:HID + P], low[:, n, :], ident[:]).then_inc(low_turned, 1)

            def ffn(n):
                pe.wait_ge(lowT_done, n + 1)
                if n == 0:
                    pe.wait_ge(bt_loaded, 16)
                else:
                    pe.wait_ge(acc_added, n)
                pe.matmul(ctx_ps[:, :], lowT[:, n % 2, :], bt_sb, start=True, stop=True).then_inc(ffn_out, 1)

            pe.wait_ge(turn_lo, NT)
            for u in range(UNITS):
                project(0, 0, 0, u)
                turn_low(u)
                if u >= 1:
                    ffn(u - 1)
            pe.wait_ge(v_taken, 1)
            turn_v(NT)
            for n in range(UNITS, NT):
                turn_low(n)
                ffn(n - 1)
            ffn(NT - 1)
            score(0, 0, 0)
            score(0, 0, 1)
            project(0, *job_of(SCORE_JOB, 0))
            score(0, 0, 2)
            score(0, 0, 3)

            def one_pass(it, final):
                for ls in range(STEPS):
                    gl, i = divmod(ls, NT)
                    in_final = final and gl == PAIR - 1
                    turns = it * (PAIR * (BLOCKS + 2)) + PRE_TURNS
                    if i in V_TURN_STEPS and not (in_final and i == 5):
                        u = turn_local(ls, 0, final) - 1
                        pe.wait_ge(turn_lo, turns + u - 1)
                        pe.wait_ge(v_taken, v_index(it, gl + (i == 5), i == 1) + 1)
                        turn_v(PRE_TURNS + u)

                    def turn(t):
                        u = turn_local(ls, t, final)
                        pe.wait_ge(turn_lo, turns + u - 1)
                        for h in range(R):
                            last = pe.transpose(turn_ps[(PRE_TURNS + u) % 2][:, h * P:(h + 1) * P],
                                                probs[:, h, t * P:(t + 1) * P], ident[:])
                        last.then_inc(turned, 1)

                    pe.wait_ge(probs_done, it * (STEPS * R) + ls * R + R)
                    turn(0)
                    if i >= 1:
                        turn(1)
                    job = job_of(ATTEND_JOB, ls)
                    if job and not (in_final and job[1] == 0):
                        project(it, *job)
                    for t in range(i + 1):
                        if t + 2 <= i:
                            turn(t + 2)
                        u, p = turn_local(ls, t, final), block_local(ls, t)
                        if t == 0:
                            pe.wait_ge(acc_added, it * STEPS + NT + ls)
                        pe.wait_ge(turn_lo, turns + u + 1)
                        slot, b = half_slot(gl, t // (NT // 2)), t % (NT // 2)
                        pe.matmul(ctx_ps[:, :], v_hi[:, slot, b, :], pT_hi[:, p % PT_SLOTS, :],
                                  start=(t == 0), stop=False)
                        pe.matmul(ctx_ps[:, :], v_lo[:, slot, b, :], pT_hi[:, p % PT_SLOTS, :],
                                  start=False, stop=False)
                        last = pe.matmul(ctx_ps[:, :], v_hi[:, slot, b, :], pT_lo[:, p % PT_SLOTS, :],
                                         start=False, stop=(t == i))
                        last.then_inc(block_summed, 1)
                    if not (final and ls == STEPS - 1):
                        score(it, ls + 1, 0)
                        score(it, ls + 1, 1)
                        job = job_of(SCORE_JOB, ls + 1)
                        if not (final and job[0] >= PAIR):
                            project(it, *job)
                        score(it, ls + 1, 2)
                        score(it, ls + 1, 3)
                    pe.wait_ge(ctx_lo_done, it * STEPS + ls + 1)
                    if i == 0:
                        pe.wait_ge(wo_split, it * (R * PAIR) + R * gl + R)
                    three(ctx_ps[:, :], [(ctx_hi[:, h * P:(h + 1) * P], ctx_lo[:, h * P:(h + 1) * P],
                                          wo_hi[:, gl % 2, h, :], wo_lo[:, gl % 2, h, :])
                                         for h in range(R)]).then_inc(out_projected, 1)

            with pe.Fori(0, PASSES - 1) as it:
                one_pass(it, False)
            one_pass(PASSES - 1, True)


def rope_tables():
    half = D // 2
    inv = (1.0 / np.float32(10000.0) ** (np.arange(half, dtype=np.float32) / np.float32(half))).astype(np.float32)
    ang = (np.arange(S, dtype=np.float32)[None, :] * inv[:, None]).astype(np.float32).astype(np.float64)
    cos, sin = np.cos(ang).astype(np.float32), np.sin(ang).astype(np.float32)
    return np.concatenate([cos, cos]), np.concatenate([-sin, sin])


def kernel(**inputs):
    import numpy as _np
    import concourse.bacc as _bacc
    from concourse import mybir as _mybir
    from concourse.bass_utils import run_bass_kernel_spmd as _run

    nc = _bacc.Bacc("TRN2", target_bir_lowering=False, num_devices=1, dynamic_dma_scratch_size=1024)
    a = {k[3:]: _np.asarray(v) for k, v in inputs.items()}
    cos_t, sin_t = rope_tables()
    per_group = [a["attn_bk"].reshape(G, 1, D), a["attn_bv"].reshape(G, 1, D), a["attn_bq"].reshape(G, R, D)]
    arrays = {
        "x": a["attn_hidden_states"], "wq": a["attn_Wq"], "wk": a["attn_Wk"], "wv": a["attn_Wv"],
        "wo": a["attn_Wo"],
        "biases": _np.concatenate(per_group, axis=1).transpose(2, 0, 1),
        "bo": a["attn_bo"], "cos_t": cos_t, "sin_t": sin_t,
        "aw": _np.concatenate([a["ffn_A"].reshape(ER, HID), a["ffn_Wr"]]).transpose(1, 0),
        "b_t": a["ffn_B"].transpose(0, 2, 1).reshape(ER, HID),
        "br": a["ffn_br"],
    }
    arrays = {k: _np.ascontiguousarray(v) for k, v in arrays.items()}
    args = [nc.dram_tensor(k, v.shape, _mybir.dt.from_np(v.dtype), kind="ExternalInput").ap()
            for k, v in arrays.items()]
    out = nc.dram_tensor("out", (1, S, HID), _mybir.dt.float32, kind="ExternalOutput").ap()
    build(nc, *args, out)
    r = _run(nc, [arrays], core_ids=[0])
    return r.results[0]["out"]
```

```python
from contextlib import ExitStack

import numpy as np

import concourse.bass as bass
from concourse import mybir

F32 = mybir.dt.float32
F32R = mybir.dt.float32r
BF16 = mybir.dt.bfloat16
ALU = mybir.AluOpType
ACT = mybir.ActivationFunctionType
AX = mybir.AxisListType

P = 128
S, HID = 1024, 512
H, G, D = 32, 8, 128
R = H // G
E, RANK = 8, 16
ER = E * RANK
KT = HID // P
NT = S // P
HALF = S // 2
BLOCKS = NT * (NT + 1) // 2
EPS = 1e-5
SCALE = float(D) ** -0.5
FFN_SCALE = 2.0 * E
MASKED = -1e30
UNITS = 2 + R
K_UNIT, V_UNIT, Q_UNIT = 0, 1, 2
PAIR = 2
PASSES = G // PAIR
STEPS = PAIR * NT
PT_SLOTS = 3
PRE_TURNS = NT + 1
V_TURN = 6

V_TURN_STEPS = (2, 6)
SPLIT_UNITS = {2: (0, 1), 3: (2, 3), 4: (4, 5)}
SPLIT_WO = {4: 0, 5: 1, 6: 2, 7: 3}


def gap_job(ls, gap, final=False):
    gl, i = divmod(ls, NT)
    k, part = {(0, "A"): (0, 0), (0, "B"): (0, 1), (0, "C"): (1, 0),
               (1, "A"): (1, 1), (1, "B"): (2, 0), (1, "C"): (2, 1)}[i % 2, gap]
    c, unit = divmod(3 * (i // 2) + k, UNITS)
    job = (gl + c, 1 - c, unit)
    return None if final and job[0] >= PAIR else (job, part)


def ended_job(ls, gap, final=False):
    found = gap_job(ls, gap, final)
    return found[0] if found and found[1] == 1 else None


def job_index(it, gl, c, unit):
    return it * (2 * UNITS * PAIR) + 2 * UNITS * gl + UNITS * c + unit


def rope_index(it, gl, c, unit):
    return it * (2 * (UNITS - 1) * PAIR) + 2 * (UNITS - 1) * gl + (UNITS - 1) * c + max(0, unit - 1)


def v_index(it, gl, c):
    return it * (2 * PAIR) + 2 * gl + c


def turn_local(ls, t, final):
    gl, i = divmod(ls, NT)
    in_final = final and gl == PAIR - 1
    return gl * (BLOCKS + 2) + i * (i + 1) // 2 + t + (i >= V_TURN_STEPS[0]) + (i >= V_TURN_STEPS[1] and not in_final)


def x_turn(n):
    return n + (n >= V_TURN)


def block_local(ls, t):
    gl, i = divmod(ls, NT)
    return gl * BLOCKS + i * (i + 1) // 2 + t


def half_slot(gl, c):
    return 2 if c else gl % 2


def build(nc, x, wq, wk, wv, wo, biases, bo, cos_t, sin_t, aw, b_t, br, out):
    x_v = x.rearrange("a (n p) d -> p (a n) d", p=P)
    out_v = out.rearrange("a (n p) d -> p (a n) d", p=P)
    w_v = {K_UNIT: wk.rearrange("(k p) n -> p k n", p=P),
           V_UNIT: wv.rearrange("(k p) n -> p k n", p=P),
           Q_UNIT: wq.rearrange("(k p) n -> p k n", p=P)}
    aw_v = aw.rearrange("(k p) n -> p k n", p=P)

    with ExitStack() as ctx:
        def sb(name, shape, dt=F32):
            return ctx.enter_context(nc.sbuf_tensor(name, shape, dt))

        def ps(name, shape):
            return ctx.enter_context(nc.psum_tensor(name, shape, F32))

        def sem(name):
            return ctx.enter_context(nc.semaphore(name))

        xT_hi = sb("xT_hi", [P, KT, S], F32R)
        xT_lo = sb("xT_lo", [P, KT, S], F32R)
        kT_hi = sb("kT_hi", [P, 3, HALF], F32R)
        kT_lo = sb("kT_lo", [P, 3, HALF], F32R)
        v_hi = sb("v_hi", [P, 3, HALF // P, D], F32R)
        v_lo = sb("v_lo", [P, 3, HALF // P, D], F32R)
        qT_hi = sb("qT_hi", [P, R, S], F32R)
        qT_lo = sb("qT_lo", [P, R, S], F32R)
        w_hi = sb("w_hi", [P, UNITS, KT, D], F32R)
        w_lo = sb("w_lo", [P, UNITS, KT, D], F32R)
        wo_hi = sb("wo_hi", [P, 2, R, HID], F32R)
        wo_lo = sb("wo_lo", [P, 2, R, HID], F32R)
        w_stage = sb("w_stage", [P, 2, KT, D])
        wo_stage = sb("wo_stage", [P, 2, HID])
        cos_sb = sb("cos_sb", [P, S])
        sin_sb = sb("sin_sb", [P, S])
        acc = sb("acc", [P, NT, HID])
        probs = sb("probs", [P, R, S])
        pT_hi = sb("pT_hi", [P, PT_SLOTS, R * P], F32R)
        pT_lo = sb("pT_lo", [P, PT_SLOTS, R * P], F32R)
        rot = sb("rot", [P, 2, HALF])
        straight = sb("straight", [P, 2, HALF])
        vT = sb("vT", [P, HALF])
        ctx_hi = sb("ctx_hi", [P, R * P], F32R)
        ctx_lo = sb("ctx_lo", [P, R * P], F32R)
        bias_all = sb("bias_all", [P, G, UNITS])
        bias_now = sb("bias_now", [P, 2, UNITS])
        ident = sb("ident", [P, P])
        ident_b = sb("ident_b", [P, P], BF16)
        mask_b = sb("mask_b", [P, P], BF16)
        neg_max = sb("neg_max", [P, R])
        exp_bias = sb("exp_bias", [P, R])
        row_sum = sb("row_sum", [P, R])
        row_inv = sb("row_inv", [P, R])
        stats = sb("stats", [P, NT, 6])
        mean_var = sb("mean_var", [P, NT, 2])
        std = sb("std", [P, NT])
        rstd = sb("rstd", [P, NT])
        logits = sb("logits", [P, NT, E])
        br_sb = sb("br_sb", [P, E])
        gate_neg = sb("gate_neg", [P, NT])
        gate_sum = sb("gate_sum", [P, NT])
        gate_inv = sb("gate_inv", [P, NT])
        aw_sb = sb("aw_sb", [P, KT, ER + E])
        xn = probs[:, 0, :].rearrange("p (b d) -> p b d", b=2)
        xT_f = probs[:, 1, :].rearrange("p (b k t) -> p b k t", b=2, k=KT)
        low = probs[:, 2, :].rearrange("p (n e) -> p n e", e=ER)
        bo_sb = probs[:, 3, HID:2 * HID]
        lowT = w_stage.rearrange("p s n t -> p (s n) t")
        bt_sb = vT[:, :]
        score_ps = [ps("score0", [P, S]), ps("score1", [P, S])]
        turn_ps = [ps("turn0", [P, HID]), ps("turn1", [P, HID])]
        ctx_ps = ps("ctx", [P, HID])
        proj_ps = ps("proj", [P, HALF])

        ffn_ps = [ctx_ps[:, :], score_ps[0][:, HID:S], score_ps[1][:, HID:S]]

        x_loaded = [sem("x_loaded0"), sem("x_loaded1")]
        aw_loaded, bias_loaded, br_loaded = sem("aw_loaded"), sem("bias_loaded"), sem("br_loaded")
        cos_loaded, sin_loaded = sem("cos_loaded"), sem("sin_loaded")
        bt_loaded, bo_loaded = sem("bt_loaded"), sem("bo_loaded")
        w_loaded = [sem("w_loaded0"), sem("w_loaded1")]
        wo_loaded = [sem("wo_loaded0"), sem("wo_loaded1")]
        out_stored = sem("out_stored")
        turned = sem("turned")
        scored = sem("scored")
        projected = sem("projected")
        block_summed = sem("block_summed")
        out_projected = sem("out_projected")
        gated_in = sem("gated_in")
        low_turned = sem("low_turned")
        ffn_out = sem("ffn_out")
        turn_hi = sem("turn_hi")
        exps = sem("exps")
        v_taken = sem("v_taken")
        swapped = sem("swapped")
        ctx_hi_done = sem("ctx_hi_done")
        std_done = sem("std_done")
        xT_f_done = sem("xT_f_done")
        gate_exp = sem("gate_exp")
        lowT_done = sem("lowT_done")
        turn_lo = sem("turn_lo")
        max_done = sem("max_done")
        bias_done = sem("bias_done")
        inv_done = sem("inv_done")
        probs_done = sem("probs_done")
        cos_done = sem("cos_done")
        ctx_lo_done = sem("ctx_lo_done")
        acc_added = sem("acc_added")
        stats_done, mean_done, var_done, rstd_done = (sem(f"{x}_done") for x in ("stats", "mean", "var", "rstd"))
        xn_done = sem("xn_done")
        low_read = sem("low_read")
        gate_step = sem("gate_step")
        const_step = sem("const_step")
        consts_done = sem("consts_done")
        w_hi_done, w_split = sem("w_hi_done"), sem("w_split")
        wo_hi_done, wo_split = sem("wo_hi_done"), sem("wo_split")
        biases_set = sem("biases_set")
        bo_added = sem("bo_added")
        sin_done, rope_summed, rope_hi = sem("sin_done"), sem("rope_summed"), sem("rope_hi")
        roped = sem("roped")

        block = ctx.enter_context(nc.Block())

        def split_dst(gl, c, unit):
            if unit == K_UNIT:
                return kT_hi[:, half_slot(gl, c), :], kT_lo[:, half_slot(gl, c), :]
            h = unit - Q_UNIT
            return qT_hi[:, h, c * HALF:(c + 1) * HALF], qT_lo[:, h, c * HALF:(c + 1) * HALF]

        @block.sync
        def _(sp):
            def load_unit(g, u):
                view = w_v[min(u, Q_UNIT)]
                col = g * (R * D) + (u - Q_UNIT) * D if u >= Q_UNIT else g * D
                sp.dma_start(w_stage[:, u % 2], view[:, :, bass.ds(col, D)]).then_inc(w_loaded[u % 2], 16)

            def load_wo(g, h):
                sp.dma_start(wo_stage[:, h % 2, :], wo[bass.ds(g * (R * D) + h * D, D), :])\
                    .then_inc(wo_loaded[h % 2], 16)

            def load_x(c):
                sp.dma_start(acc[:, c * NT // 2:(c + 1) * NT // 2, :],
                             x_v[:, c * NT // 2:(c + 1) * NT // 2, :]).then_inc(x_loaded[c], 16)

            load_x(0)
            load_unit(0, 0)
            load_unit(0, 1)
            load_x(1)
            load_wo(0, 0)
            load_wo(0, 1)
            for u in range(2, UNITS):
                sp.wait_ge(w_split, u - 1)
                load_unit(0, u)
            for h in range(2, R):
                sp.wait_ge(wo_split, h - 1)
                load_wo(0, h)
            sp.wait_ge(turned, V_TURN + 1)
            sp.dma_start(bt_sb, b_t).then_inc(bt_loaded, 16)
            sp.wait_ge(ffn_out, NT)

            def one_pass(it, final):
                for gl in range(PAIR):
                    if final and gl == PAIR - 1:
                        break
                    for u in range(UNITS):
                        sp.wait_ge(w_split, it * (UNITS * PAIR) + UNITS * (gl + 1) + u - 1)
                        load_unit(it * PAIR + gl + 1, u)
                    for h in range(R):
                        sp.wait_ge(wo_split, it * (R * PAIR) + R * (gl + 1) + h - 1)
                        load_wo(it * PAIR + gl + 1, h)

            with sp.Fori(0, PASSES - 1) as it:
                one_pass(it, False)
            one_pass(PASSES - 1, True)
            for i in range(NT):
                sp.wait_ge(acc_added, NT + (G - 1) * NT + i + 1)
                sp.dma_start(out_v[:, i, :], acc[:, i, :]).then_inc(out_stored, 16)
            sp.wait_ge(out_stored, 16 * NT)

        @block.gpsimd
        def _(pool):
            def split_unit(it, gl, u):
                n = it * (UNITS * PAIR) + UNITS * gl + u
                pool.wait_ge(w_hi_done, n + 1)
                pool.tensor_tensor(w_lo[:, u], w_stage[:, u % 2], w_hi[:, u].bitcast(F32),
                                   ALU.subtract).then_inc(w_split, 1)

            def split_wo(it, gl, h):
                n = it * (R * PAIR) + R * gl + h
                pool.wait_ge(wo_hi_done, n + 1)
                pool.tensor_tensor(wo_lo[:, gl % 2, h, :], wo_stage[:, h % 2, :],
                                   wo_hi[:, gl % 2, h, :].bitcast(F32), ALU.subtract).then_inc(wo_split, 1)

            def rope(it, gl, c, unit, times_sin=True):
                n = rope_index(it, gl, c, unit)
                b = rope_index(0, gl, c, unit) % 2
                hi, lo = split_dst(gl, c, unit)
                if times_sin:
                    pool.wait_ge(swapped, (n + 1) * 2)
                    pool.tensor_tensor(rot[:, b], rot[:, b], sin_sb[:, c * HALF:(c + 1) * HALF],
                                       ALU.mult).then_inc(sin_done, 1)
                pool.wait_ge(sin_done, n + 1)
                pool.wait_ge(cos_done, n + 1)
                pool.tensor_tensor(hi, straight[:, b], rot[:, b], ALU.add).then_inc(rope_hi, 1)
                pool.wait_ge(rope_hi, n + 1)
                pool.tensor_tensor(straight[:, b], straight[:, b], rot[:, b], ALU.add).then_inc(rope_summed, 1)
                pool.wait_ge(rope_summed, n + 1)
                pool.tensor_tensor(lo, straight[:, b], hi.bitcast(F32), ALU.subtract).then_inc(roped, 1)

            def set_biases(g, slot):
                pool.tensor_copy(bias_now[:, slot:slot + 1, :], bias_all[:, bass.ds(g, 1), :]).then_inc(biases_set, 1)

            pool.memset(ident[:], 0.0).then_inc(const_step, 1)
            pool.memset(ident_b[:], 0.0).then_inc(const_step, 1)
            pool.memset(mask_b[:], 0.0).then_inc(const_step, 1)
            pool.wait_ge(const_step, 3)
            for tile in (ident, ident_b):
                pool.affine_select(out=tile[:], in_=tile[:], compare_op=ALU.not_equal, fill=1.0, base=0,
                                   pattern=[[-1, P]], channel_multiplier=1).then_inc(consts_done, 1)
            pool.affine_select(out=mask_b[:], in_=mask_b[:], compare_op=ALU.is_ge, fill=MASKED, base=0,
                               pattern=[[-1, P]], channel_multiplier=1).then_inc(consts_done, 1)
            pool.wait_ge(bias_loaded, 16)
            set_biases(0, 0)
            pool.wait_ge(bo_loaded, 16)

            def add_bo(n):
                pool.wait_ge(xn_done, n + 1)
                pool.tensor_tensor(acc[:, n, :], acc[:, n, :], bo_sb, ALU.add).then_inc(bo_added, 1)

            for n in range(4):
                add_bo(n)
            pool.wait_ge(sin_loaded, 16)
            for n, u in enumerate((K_UNIT, *range(Q_UNIT, UNITS))):
                rope(0, 0, 0, u, times_sin=False)
                if 4 + n < NT:
                    add_bo(4 + n)
            rope(0, *ended_job(0, "B"))

            def one_pass(it, final):
                for ls in range(STEPS):
                    gl, i = divmod(ls, NT)
                    in_final = final and gl == PAIR - 1
                    job = ended_job(ls, "C", final)
                    if job and job[2] != V_UNIT:
                        rope(it, *job)
                    if not in_final:
                        for u in SPLIT_UNITS.get(i, ()):
                            split_unit(it, gl + 1, u)
                        if i == 1:
                            set_biases(it * PAIR + gl + 1, (gl + 1) % 2)
                        if i in SPLIT_WO:
                            split_wo(it, gl + 1, SPLIT_WO[i])
                    if final and ls == STEPS - 1:
                        break
                    for gap in "AB":
                        job = ended_job(ls + 1, gap, final)
                        if job and job[2] != V_UNIT:
                            rope(it, *job)

            with pool.Fori(0, PASSES - 1) as it:
                one_pass(it, False)
            one_pass(PASSES - 1, True)

        @block.scalar
        def _(act):
            def take_job(it, gl, c, unit):
                act.wait_ge(projected, job_index(it, gl, c, unit) + 1)
                bias = bias_now[:, gl % 2, unit:unit + 1]
                if unit == V_UNIT:
                    act.activation(vT[:, :], proj_ps[:, :], ACT.Identity, bias=bias).then_inc(v_taken, 1)
                    return
                n = rope_index(it, gl, c, unit)
                b = rope_index(0, gl, c, unit) % 2
                if not (isinstance(n, int) and n < 2):
                    act.wait_ge(rope_summed, n - 1)
                m = D // 2
                act.activation(rot[0:m, b, :], proj_ps[m:D, :], ACT.Identity, bias=bias[m:D]).then_inc(swapped, 1)
                act.activation(rot[m:D, b, :], proj_ps[0:m, :], ACT.Identity, bias=bias[0:m]).then_inc(swapped, 1)

            def exp_head(it, ls, h):
                n = it * (STEPS * R) + ls * R + h
                w = (ls % NT + 1) * P
                act.wait_ge(bias_done, n + 1)
                act.activation(probs[:, h, 0:w], score_ps[h % 2][:, 0:w], ACT.Exp, bias=exp_bias[:, h:h + 1],
                               scale=SCALE, accum_out=row_sum[:, h:h + 1]).then_inc(exps, 1)

            def v_turn_hi(it, ls, final):
                u = turn_local(ls, 0, final) - 1
                gl, i = divmod(ls, NT)
                slot = half_slot(gl + (i == V_TURN_STEPS[1]), i == V_TURN_STEPS[0])
                act.wait_ge(turned, it * (PAIR * (BLOCKS + 2)) + PRE_TURNS + u + 1)
                act.activation(v_hi[:, slot].rearrange("p b d -> p (b d)"), turn_ps[(PRE_TURNS + u) % 2][:, :],
                               ACT.Copy).then_inc(turn_hi, 1)

            act.dma_start(aw_sb[:], aw_v).then_inc(aw_loaded, 16)
            act.dma_start(bias_all[:], biases).then_inc(bias_loaded, 16)
            act.dma_start(br_sb[:], br.partition_broadcast(P)).then_inc(br_loaded, 16)
            act.dma_start(cos_sb[:], cos_t).then_inc(cos_loaded, 16)
            act.dma_start(sin_sb[:], sin_t).then_inc(sin_loaded, 16)
            act.dma_start(bo_sb, bo.partition_broadcast(P)).then_inc(bo_loaded, 16)

            def take_std(c):
                act.wait_ge(var_done, c + 1)
                tiles = slice(c * NT // 2, (c + 1) * NT // 2)
                act.activation(std[:, tiles], std[:, tiles], ACT.Sqrt).then_inc(std_done, 1)

            def take_x(n):
                u = x_turn(n)
                act.wait_ge(turned, u + 1)
                if n >= 2:
                    act.wait_ge(gated_in, n - 1)
                src = turn_ps[u % 2][:, :].rearrange("p (k t) -> p k t", k=KT)
                act.activation(xT_f[:, n % 2], src, ACT.Copy).then_inc(xT_f_done, 1)
                act.activation(xT_hi[:, :, n * P:(n + 1) * P], src, ACT.Copy).then_inc(turn_hi, 1)

            take_std(0)
            for n in range(4):
                take_x(n)
            take_std(1)
            act.wait_ge(biases_set, 1)
            take_job(0, 0, 0, K_UNIT)
            take_x(4)
            take_job(0, 0, 0, V_UNIT)
            take_x(5)
            take_job(0, 0, 0, Q_UNIT)
            act.wait_ge(turned, V_TURN + 1)
            act.activation(v_hi[:, 0].rearrange("p b d -> p (b d)"), turn_ps[V_TURN % 2][:, :],
                           ACT.Copy).then_inc(turn_hi, 1)
            take_x(6)
            take_job(0, 0, 0, Q_UNIT + 1)
            take_x(7)
            take_job(0, 0, 0, Q_UNIT + 2)
            act.wait_ge(gate_step, 3)
            act.activation(logits[:], logits[:], ACT.Exp).then_inc(gate_exp, 1)
            take_job(0, 0, 0, Q_UNIT + 3)
            for b in range(2):
                act.wait_ge(low_turned, b + 1)
                act.activation(lowT[:, b * 4:(b + 1) * 4, :].rearrange("p n t -> p (n t)"), score_ps[b][:, HID:S],
                               ACT.Copy).then_inc(lowT_done, 1)
            for h in range(R):
                exp_head(0, 0, h)
            take_job(0, *ended_job(0, "B"))

            def one_pass(it, final):
                for ls in range(STEPS):
                    gl, i = divmod(ls, NT)
                    in_final = final and gl == PAIR - 1
                    if i in V_TURN_STEPS and not (in_final and i == V_TURN_STEPS[1]):
                        v_turn_hi(it, ls, final)
                    for t in range(i + 1):
                        u, p = turn_local(ls, t, final), block_local(ls, t)
                        act.wait_ge(turned, it * (PAIR * (BLOCKS + 2)) + PRE_TURNS + u + 1)
                        act.wait_ge(block_summed, it * (PAIR * BLOCKS) + p + 1)
                        act.activation(pT_hi[:, p % PT_SLOTS, :], turn_ps[(PRE_TURNS + u) % 2][:, :],
                                       ACT.Copy).then_inc(turn_hi, 1)
                        if t == min(i, 1):
                            job = ended_job(ls, "C", final)
                            if job:
                                take_job(it, *job)
                    act.wait_ge(block_summed, it * (PAIR * BLOCKS) + block_local(ls, i) + 1 + PT_SLOTS)
                    act.activation(ctx_hi[:], ctx_ps[:, :], ACT.Copy).then_inc(ctx_hi_done, 1)
                    if final and ls == STEPS - 1:
                        break
                    exp_head(it, ls + 1, 0)
                    exp_head(it, ls + 1, 1)
                    job = ended_job(ls + 1, "A", final)
                    if job:
                        take_job(it, *job)
                    exp_head(it, ls + 1, 2)
                    exp_head(it, ls + 1, 3)
                    job = ended_job(ls + 1, "B", final)
                    if job:
                        if job[2] == K_UNIT:
                            act.wait_ge(biases_set, it * PAIR + job[0] + 1)
                        take_job(it, *job)

            with act.Fori(0, PASSES - 1) as it:
                one_pass(it, False)
            one_pass(PASSES - 1, True)

        @block.vector
        def _(dve):
            def lo_part(out_lo, src_ps, hi):
                return dve.tensor_tensor(out_lo, src_ps, hi.bitcast(F32), ALU.subtract)

            def times_cos(it, gl, c, unit):
                n = rope_index(it, gl, c, unit)
                b = rope_index(0, gl, c, unit) % 2
                dve.wait_ge(swapped, (n + 1) * 2)
                if not (isinstance(n, int) and n < 2):
                    dve.wait_ge(roped, n - 1)
                dve.scalar_tensor_tensor(straight[:, b], proj_ps[:, :], bias_now[:, gl % 2, unit:unit + 1],
                                         cos_sb[:, c * HALF:(c + 1) * HALF], ALU.add, ALU.mult)\
                    .then_inc(cos_done, 1)

            def row_max(it, ls, h):
                n = it * (STEPS * R) + ls * R + h
                w = (ls % NT + 1) * P
                dve.wait_ge(scored, n + 1)
                dve.tensor_reduce(neg_max[:, h:h + 1], score_ps[h % 2][:, 0:w], AX.X, ALU.max).then_inc(max_done, 1)
                dve.wait_ge(max_done, n + 1)
                dve.tensor_scalar(exp_bias[:, h:h + 1], neg_max[:, h:h + 1], -SCALE, None, ALU.mult)\
                    .then_inc(bias_done, 1)

            def normalise(it, ls, h):
                n = it * (STEPS * R) + ls * R + h
                w = (ls % NT + 1) * P
                dve.wait_ge(exps, n + 1)
                dve.reciprocal(row_inv[:, h:h + 1], row_sum[:, h:h + 1]).then_inc(inv_done, 1)
                dve.wait_ge(inv_done, n + 1)
                dve.tensor_scalar(probs[:, h, 0:w], probs[:, h, 0:w], row_inv[:, h:h + 1], None, ALU.mult)\
                    .then_inc(probs_done, 1)

            def score_part(it, ls, final=False, ctx_step=False):
                row_max(it, ls, 0)
                if ctx_step:
                    dve.wait_ge(ctx_hi_done, it * STEPS + ls)
                    lo_part(ctx_lo[:], ctx_ps[:, :], ctx_hi[:]).then_inc(ctx_lo_done, 1)
                row_max(it, ls, 1)
                normalise(it, ls, 0)
                normalise(it, ls, 1)
                job = ended_job(ls, "A", final)
                if job and job[2] != V_UNIT:
                    times_cos(it, *job)
                row_max(it, ls, 2)
                row_max(it, ls, 3)
                normalise(it, ls, 2)
                normalise(it, ls, 3)
                job = ended_job(ls, "B", final)
                if job and job[2] != V_UNIT:
                    times_cos(it, *job)

            def unit_hi(it, gl, u):
                dve.wait_ge(w_loaded[u % 2], (it * (UNITS * PAIR // 2) + UNITS // 2 * gl + u // 2 + 1) * 16)
                dve.tensor_copy(w_hi[:, u], w_stage[:, u % 2]).then_inc(w_hi_done, 1)

            def rows_hi(it, gl, h):
                dve.wait_ge(wo_loaded[h % 2], (it * (R * PAIR // 2) + R // 2 * gl + h // 2 + 1) * 16)
                dve.tensor_copy(wo_hi[:, gl % 2, h, :], wo_stage[:, h % 2, :]).then_inc(wo_hi_done, 1)

            def stats_of(c):
                tiles = slice(c * NT // 2, (c + 1) * NT // 2)
                dve.wait_ge(x_loaded[c], 16)
                for n in range(c * NT // 2, (c + 1) * NT // 2):
                    dve.bn_stats(stats[:, n, :], acc[:, n, :]).then_inc(stats_done, 1)
                for n in range(c * NT // 2, (c + 1) * NT // 2):
                    dve.wait_ge(stats_done, n + 1)
                    dve.bn_aggr(mean_var[:, n, :], stats[:, n, :]).then_inc(mean_done, 1)
                dve.wait_ge(mean_done, (c + 1) * NT // 2)
                dve.tensor_scalar(std[:, tiles], mean_var[:, tiles, 1], EPS, None, ALU.add).then_inc(var_done, 1)
                dve.wait_ge(std_done, c + 1)
                dve.reciprocal(rstd[:, tiles], std[:, tiles]).then_inc(rstd_done, 1)
                dve.wait_ge(rstd_done, c + 1)

            def normal_x(n):
                if n >= 2:
                    dve.wait_ge(turned, x_turn(n - 2) + 1)
                dve.tensor_scalar(xn[:, n % 2], acc[:, n, :], mean_var[:, n, 0:1], rstd[:, n:n + 1],
                                  ALU.subtract, ALU.mult).then_inc(xn_done, 1)

            def x_lo(n):
                u = x_turn(n)
                dve.wait_ge(turn_hi, u + 1)
                lo_part(xT_lo[:, :, n * P:(n + 1) * P],
                        turn_ps[u % 2][:, :].rearrange("p (k t) -> p k t", k=KT),
                        xT_hi[:, :, n * P:(n + 1) * P]).then_inc(turn_lo, 1)

            def take_low(n):
                dve.wait_ge(gated_in, n + 1)
                dve.tensor_copy(logits[:, n, :], score_ps[n % 2][:, ER:ER + E]).then_inc(low_read, 1)
                dve.tensor_copy(low[:, n, :], score_ps[n % 2][:, 0:ER]).then_inc(low_read, 1)

            def first_unit(u):
                unit_hi(0, 0, u)
                dve.wait_ge(w_hi_done, u + 1)
                dve.tensor_tensor(w_lo[:, u], w_stage[:, u % 2], w_hi[:, u].bitcast(F32),
                                  ALU.subtract).then_inc(w_split, 1)

            def first_rows(h):
                rows_hi(0, 0, h)
                dve.wait_ge(wo_hi_done, h + 1)
                dve.tensor_tensor(wo_lo[:, 0, h, :], wo_stage[:, h % 2, :], wo_hi[:, 0, h, :].bitcast(F32),
                                  ALU.subtract).then_inc(wo_split, 1)

            def first_rope(unit):
                times_cos(0, 0, 0, unit)
                b = rope_index(0, 0, 0, unit) % 2
                dve.tensor_tensor(rot[:, b], rot[:, b], sin_sb[:, 0:HALF], ALU.mult).then_inc(sin_done, 1)

            stats_of(0)
            normal_x(0)
            normal_x(1)
            first_unit(0)
            x_lo(0)
            normal_x(2)
            x_lo(1)
            normal_x(3)
            first_unit(1)
            take_low(0)
            x_lo(2)
            take_low(1)
            x_lo(3)
            stats_of(1)
            normal_x(4)
            normal_x(5)
            first_unit(2)
            take_low(2)
            dve.wait_ge(cos_loaded, 16)
            dve.wait_ge(sin_loaded, 16)
            dve.wait_ge(biases_set, 1)
            first_rope(K_UNIT)
            x_lo(4)
            normal_x(6)
            first_unit(3)
            take_low(3)
            x_lo(5)
            normal_x(7)
            first_unit(4)
            first_rope(Q_UNIT)
            dve.wait_ge(turn_hi, V_TURN + 1)
            lo_part(v_lo[:, 0].rearrange("p b d -> p (b d)"), turn_ps[V_TURN % 2][:, :],
                    v_hi[:, 0].rearrange("p b d -> p (b d)")).then_inc(turn_lo, 1)
            take_low(4)
            x_lo(6)
            first_unit(5)
            first_rope(Q_UNIT + 1)
            take_low(5)
            x_lo(7)
            first_rows(0)
            first_rows(1)
            first_rope(Q_UNIT + 2)
            take_low(6)
            take_low(7)
            dve.wait_ge(low_read, 2 * NT)
            dve.wait_ge(br_loaded, 16)
            dve.tensor_tensor(logits[:], logits[:], br_sb[:, None, :].to_broadcast([P, NT, E]), ALU.add)\
                .then_inc(gate_step, 1)
            dve.wait_ge(gate_step, 1)
            dve.tensor_reduce(gate_neg[:], logits[:], AX.X, ALU.max).then_inc(gate_step, 1)
            dve.wait_ge(gate_step, 2)
            dve.tensor_tensor(logits[:], logits[:], gate_neg[:, :, None].to_broadcast([P, NT, E]), ALU.subtract)\
                .then_inc(gate_step, 1)
            dve.wait_ge(gate_exp, 1)
            dve.tensor_reduce(gate_sum[:], logits[:], AX.X, ALU.add).then_inc(gate_step, 1)
            dve.wait_ge(gate_step, 4)
            dve.reciprocal(gate_inv[:], gate_sum[:]).then_inc(gate_step, 1)
            dve.wait_ge(gate_step, 5)
            dve.tensor_scalar(gate_inv[:], gate_inv[:], FFN_SCALE, None, ALU.mult).then_inc(gate_step, 1)
            dve.wait_ge(gate_step, 6)
            dve.tensor_tensor(logits[:], logits[:], gate_inv[:, :, None].to_broadcast([P, NT, E]), ALU.mult)\
                .then_inc(gate_step, 1)
            dve.wait_ge(gate_step, 7)
            low_e = low.rearrange("p n (e r) -> p (n e) r", e=E)
            dve.tensor_tensor(low_e, low_e,
                              logits[:].rearrange("p n e -> p (n e)")[:, :, None].to_broadcast([P, NT * E, RANK]),
                              ALU.mult).then_inc(gate_step, 1)

            def add_ffn(n):
                dve.wait_ge(ffn_out, n + 1)
                dve.wait_ge(bo_added, n + 1)
                dve.tensor_tensor(acc[:, n, :], ffn_ps[n % 3], acc[:, n, :], ALU.add).then_inc(acc_added, 1)

            first_rope(Q_UNIT + 3)
            row_max(0, 0, 0)
            add_ffn(0)
            add_ffn(1)
            row_max(0, 0, 1)
            normalise(0, 0, 0)
            normalise(0, 0, 1)
            add_ffn(2)
            add_ffn(3)
            row_max(0, 0, 2)
            add_ffn(4)
            add_ffn(5)
            row_max(0, 0, 3)
            normalise(0, 0, 2)
            add_ffn(6)
            add_ffn(7)
            normalise(0, 0, 3)
            times_cos(0, *ended_job(0, "B"))
            first_rows(2)
            first_rows(3)

            def one_pass(it, final):
                for ls in range(STEPS):
                    gl, i = divmod(ls, NT)
                    in_final = final and gl == PAIR - 1
                    if not in_final:
                        for u in SPLIT_UNITS.get(i, ()):
                            dve.wait_ge(projected, job_index(it, gl, 1, u) + 1)
                            unit_hi(it, gl + 1, u)
                        if i in SPLIT_WO:
                            dve.wait_ge(out_projected, it * STEPS + ls)
                            rows_hi(it, gl + 1, SPLIT_WO[i])
                    if i in V_TURN_STEPS and not (in_final and i == V_TURN_STEPS[1]):
                        u = turn_local(ls, 0, final) - 1
                        slot = half_slot(gl + (i == V_TURN_STEPS[1]), i == V_TURN_STEPS[0])
                        dve.wait_ge(turn_hi, it * (PAIR * (BLOCKS + 2)) + PRE_TURNS + u + 1)
                        lo_part(v_lo[:, slot].rearrange("p b d -> p (b d)"), turn_ps[(PRE_TURNS + u) % 2][:, :],
                                v_hi[:, slot].rearrange("p b d -> p (b d)")).then_inc(turn_lo, 1)
                    for t in range(i + 1):
                        u, p = turn_local(ls, t, final), block_local(ls, t)
                        dve.wait_ge(turn_hi, it * (PAIR * (BLOCKS + 2)) + PRE_TURNS + u + 1)
                        lo_part(pT_lo[:, p % PT_SLOTS, :], turn_ps[(PRE_TURNS + u) % 2][:, :],
                                pT_hi[:, p % PT_SLOTS, :]).then_inc(turn_lo, 1)
                        if t == min(i, 1):
                            job = ended_job(ls, "C", final)
                            if job and job[2] != V_UNIT:
                                times_cos(it, *job)
                    if final and ls == STEPS - 1:
                        dve.wait_ge(ctx_hi_done, it * STEPS + ls + 1)
                        lo_part(ctx_lo[:], ctx_ps[:, :], ctx_hi[:]).then_inc(ctx_lo_done, 1)
                    else:
                        score_part(it, ls + 1, final, ctx_step=True)
                    dve.wait_ge(out_projected, it * STEPS + ls + 1)
                    dve.tensor_tensor(acc[:, i, :], ctx_ps[:, :], acc[:, i, :], ALU.add).then_inc(acc_added, 1)

            with dve.Fori(0, PASSES - 1) as it:
                one_pass(it, False)
            one_pass(PASSES - 1, True)

        @block.tensor
        def _(pe):
            def three(out, pairs):
                n = len(pairs)
                for j, (a_hi, a_lo, b_hi, b_lo) in enumerate(pairs):
                    pe.matmul(out, a_hi, b_hi, start=(j == 0), stop=False)
                    pe.matmul(out, a_hi, b_lo, start=False, stop=False)
                    last = pe.matmul(out, a_lo, b_hi, start=False, stop=(j == n - 1))
                return last

            def project(it, job, part):
                gl, c, unit = job
                if part == 0:
                    if unit == V_UNIT + 1:
                        pe.wait_ge(v_taken, v_index(it, gl, c) + 1)
                    elif not (isinstance(it, int) and it == 0 and gl == 0 and c == 0 and unit == 0):
                        pe.wait_ge(cos_done, rope_index(it, gl, c, unit) + (unit == V_UNIT))
                    if c == 0:
                        pe.wait_ge(w_split, it * (UNITS * PAIR) + UNITS * gl + unit + 1)
                cols = slice(c * HALF, (c + 1) * HALF)
                for k in (range(KT // 2) if part == 0 else range(KT // 2, KT)):
                    pe.matmul(proj_ps[:, :], w_hi[:, unit, k, :], xT_hi[:, k, cols], start=(k == 0), stop=False)
                    pe.matmul(proj_ps[:, :], w_hi[:, unit, k, :], xT_lo[:, k, cols], start=False, stop=False)
                    last = pe.matmul(proj_ps[:, :], w_lo[:, unit, k, :], xT_hi[:, k, cols],
                                     start=False, stop=(k == KT - 1))
                if part == 1:
                    last.then_inc(projected, 1)

            def fill(it, ls, gap, final=False):
                found = gap_job(ls, gap, final)
                if found:
                    project(it, *found)

            def score(it, ls, h):
                gl, i = divmod(ls, NT)
                n = it * (STEPS * R) + ls * R + h
                if not (isinstance(n, int) and n < 2):
                    pe.wait_ge(exps, n - 1)
                if i % (NT // 2) == 0:
                    pe.wait_ge(roped, rope_index(it, gl, i // (NT // 2), Q_UNIT + h) + 1)
                w = (i + 1) * P
                q_hi, q_lo = qT_hi[:, h, i * P:(i + 1) * P], qT_lo[:, h, i * P:(i + 1) * P]
                for c in range(2 if w > HALF else 1):
                    m = max(2 * P, min(HALF, w - c * HALF))
                    o = score_ps[h % 2][:, c * HALF:c * HALF + m]
                    slot = half_slot(gl, c)
                    diagonal = w - c * HALF <= HALF
                    pe.matmul(o, q_hi, kT_hi[:, slot, 0:m], start=True, stop=False)
                    pe.matmul(o, q_hi, kT_lo[:, slot, 0:m], start=False, stop=False)
                    last = pe.matmul(o, q_lo, kT_hi[:, slot, 0:m], start=False, stop=not diagonal)
                last = pe.matmul(score_ps[h % 2][:, w - P:w], ident_b[:], mask_b[:], start=False, stop=True)
                last.then_inc(scored, 1)

            def turn_v(u):
                for b in range(HALF // P):
                    last = pe.transpose(turn_ps[u % 2][:, b * P:(b + 1) * P], vT[:, b * P:(b + 1) * P], ident[:])
                last.then_inc(turned, 1)

            pe.wait_ge(consts_done, 3)
            pe.wait_ge(aw_loaded, 16)

            def gate_in(n):
                pe.wait_ge(xT_f_done, n + 1)
                if n >= 2:
                    pe.wait_ge(low_read, 2 * (n - 1))
                for k in range(KT):
                    last = pe.matmul(score_ps[n % 2][:, 0:ER + E], xT_f[:, n % 2, k, :], aw_sb[:, k, :],
                                     start=(k == 0), stop=(k == KT - 1))
                last.then_inc(gated_in, 1)

            def turn_x(n):
                u = x_turn(n)
                pe.wait_ge(xn_done, n + 1)
                if u >= 2:
                    pe.wait_ge(turn_lo, u - 1)
                for k in range(KT):
                    last = pe.transpose(turn_ps[u % 2][:, k * P:(k + 1) * P], xn[:, n % 2, k * P:(k + 1) * P],
                                        ident[:])
                    if n == 0 and k < PT_SLOTS:
                        last.then_inc(block_summed, 1)
                last.then_inc(turned, 1)

            def first_job(unit):
                project(0, (0, 0, unit), 0)
                project(0, (0, 0, unit), 1)

            turn_x(0)
            turn_x(1)
            gate_in(0)
            turn_x(2)
            gate_in(1)
            turn_x(3)
            pe.wait_ge(turn_lo, 4)
            first_job(K_UNIT)
            gate_in(2)
            turn_x(4)
            first_job(V_UNIT)
            gate_in(3)
            turn_x(5)
            first_job(Q_UNIT)
            pe.wait_ge(v_taken, 1)
            pe.wait_ge(turn_lo, V_TURN - 1)
            turn_v(V_TURN)
            gate_in(4)
            turn_x(6)
            first_job(Q_UNIT + 1)
            gate_in(5)
            turn_x(7)
            first_job(Q_UNIT + 2)
            gate_in(6)
            gate_in(7)
            first_job(Q_UNIT + 3)
            pe.wait_ge(gate_step, 8)
            for n in range(NT):
                last = pe.transpose(score_ps[n // 4][:, HID + n % 4 * P:HID + (n % 4 + 1) * P], low[:, n, :], ident[:])
                if n % 4 == 3:
                    last.then_inc(low_turned, 1)

            def ffn(n):
                if n == 0:
                    pe.wait_ge(bt_loaded, 16)
                    pe.wait_ge(lowT_done, 1)
                if n == 2:
                    pe.wait_ge(lowT_done, 2)
                if n >= 3:
                    pe.wait_ge(acc_added, n - 2)
                pe.matmul(ffn_ps[n % 3], lowT[:, n, :], bt_sb, start=True, stop=True).then_inc(ffn_out, 1)

            score(0, 0, 0)
            ffn(0)
            ffn(1)
            score(0, 0, 1)
            pe.wait_ge(turn_lo, PRE_TURNS)
            fill(0, 0, "A")
            ffn(2)
            ffn(3)
            score(0, 0, 2)
            ffn(4)
            ffn(5)
            score(0, 0, 3)
            ffn(6)
            ffn(7)
            fill(0, 0, "B")

            def one_pass(it, final):
                for ls in range(STEPS):
                    gl, i = divmod(ls, NT)
                    in_final = final and gl == PAIR - 1
                    turns = it * (PAIR * (BLOCKS + 2)) + PRE_TURNS
                    if i in V_TURN_STEPS and not (in_final and i == V_TURN_STEPS[1]):
                        u = turn_local(ls, 0, final) - 1
                        pe.wait_ge(turn_lo, turns + u - 1)
                        pe.wait_ge(v_taken, v_index(it, gl + (i == V_TURN_STEPS[1]), i == V_TURN_STEPS[0]) + 1)
                        turn_v(PRE_TURNS + u)

                    def turn(t):
                        u = turn_local(ls, t, final)
                        pe.wait_ge(turn_lo, turns + u - 1)
                        for h in range(R):
                            last = pe.transpose(turn_ps[(PRE_TURNS + u) % 2][:, h * P:(h + 1) * P],
                                                probs[:, h, t * P:(t + 1) * P], ident[:])
                        last.then_inc(turned, 1)

                    pe.wait_ge(probs_done, it * (STEPS * R) + ls * R + R)
                    turn(0)
                    if i >= 1:
                        turn(1)
                    fill(it, ls, "C", final)
                    last_step = final and ls == STEPS - 1
                    for t in range(i + 1):
                        if t == i and not last_step:
                            score(it, ls + 1, 0)
                        if t + 2 <= i:
                            turn(t + 2)
                        u, p = turn_local(ls, t, final), block_local(ls, t)
                        if t == 0:
                            pe.wait_ge(acc_added, it * STEPS + NT + ls)
                        pe.wait_ge(turn_lo, turns + u + 1)
                        slot, b = half_slot(gl, t // (NT // 2)), t % (NT // 2)
                        pe.matmul(ctx_ps[:, :], v_hi[:, slot, b, :], pT_hi[:, p % PT_SLOTS, :],
                                  start=(t == 0), stop=False)
                        pe.matmul(ctx_ps[:, :], v_lo[:, slot, b, :], pT_hi[:, p % PT_SLOTS, :],
                                  start=False, stop=False)
                        last = pe.matmul(ctx_ps[:, :], v_hi[:, slot, b, :], pT_lo[:, p % PT_SLOTS, :],
                                         start=False, stop=(t == i))
                        last.then_inc(block_summed, 1)
                    if not last_step:
                        score(it, ls + 1, 1)
                        fill(it, ls + 1, "A", final)
                        score(it, ls + 1, 2)
                        score(it, ls + 1, 3)
                        if i % 2 == 1:
                            fill(it, ls + 1, "B", final)
                    pe.wait_ge(ctx_lo_done, it * STEPS + ls + 1)
                    if i == 0:
                        pe.wait_ge(wo_split, it * (R * PAIR) + R * gl + R)
                    three(ctx_ps[:, :], [(ctx_hi[:, h * P:(h + 1) * P], ctx_lo[:, h * P:(h + 1) * P],
                                          wo_hi[:, gl % 2, h, :], wo_lo[:, gl % 2, h, :])
                                         for h in range(R)]).then_inc(out_projected, 1)
                    if i % 2 == 0:
                        fill(it, ls + 1, "B", final)

            with pe.Fori(0, PASSES - 1) as it:
                one_pass(it, False)
            one_pass(PASSES - 1, True)


def rope_tables():
    half = D // 2
    inv = (1.0 / np.float32(10000.0) ** (np.arange(half, dtype=np.float32) / np.float32(half))).astype(np.float32)
    ang = (np.arange(S, dtype=np.float32)[None, :] * inv[:, None]).astype(np.float32).astype(np.float64)
    cos, sin = np.cos(ang).astype(np.float32), np.sin(ang).astype(np.float32)
    return np.concatenate([cos, cos]), np.concatenate([-sin, sin])


def kernel(**inputs):
    import numpy as _np
    import concourse.bacc as _bacc
    from concourse import mybir as _mybir
    from concourse.bass_utils import run_bass_kernel_spmd as _run

    nc = _bacc.Bacc("TRN2", target_bir_lowering=False, num_devices=1, dynamic_dma_scratch_size=1024)
    a = {k[3:]: _np.asarray(v) for k, v in inputs.items()}
    cos_t, sin_t = rope_tables()
    per_group = [a["attn_bk"].reshape(G, 1, D), a["attn_bv"].reshape(G, 1, D), a["attn_bq"].reshape(G, R, D)]
    arrays = {
        "x": a["attn_hidden_states"], "wq": a["attn_Wq"], "wk": a["attn_Wk"], "wv": a["attn_Wv"],
        "wo": a["attn_Wo"],
        "biases": _np.concatenate(per_group, axis=1).transpose(2, 0, 1),
        "bo": a["attn_bo"], "cos_t": cos_t, "sin_t": sin_t,
        "aw": _np.concatenate([a["ffn_A"].reshape(ER, HID), a["ffn_Wr"]]).transpose(1, 0),
        "b_t": a["ffn_B"].transpose(0, 2, 1).reshape(ER, HID),
        "br": a["ffn_br"],
    }
    arrays = {k: _np.ascontiguousarray(v) for k, v in arrays.items()}
    args = [nc.dram_tensor(k, v.shape, _mybir.dt.from_np(v.dtype), kind="ExternalInput").ap()
            for k, v in arrays.items()]
    out = nc.dram_tensor("out", (1, S, HID), _mybir.dt.float32, kind="ExternalOutput").ap()
    build(nc, *args, out)
    r = _run(nc, [arrays], core_ids=[0])
    return r.results[0]["out"]
```

```python
from contextlib import ExitStack

import numpy as np

import concourse.bass as bass
from concourse import mybir

F32 = mybir.dt.float32
F32R = mybir.dt.float32r
ALU = mybir.AluOpType
ACT = mybir.ActivationFunctionType
AX = mybir.AxisListType

P = 128
S, HID = 1024, 512
H, G, D = 32, 8, 128
R = H // G
E, RANK = 8, 16
ER = E * RANK
KT = HID // P
NT = S // P
HALF = S // 2
BLOCKS = NT * (NT + 1) // 2
EPS = 1e-5
ROOT_SCALE = float(D) ** -0.25
FFN_SCALE = 2.0 * E
MASKED = -1e30
UNITS = 2 + R
K_UNIT, V_UNIT, Q_UNIT = 0, 1, 2
PAIR = 2
PASSES = G // PAIR
STEPS = PAIR * NT
PT_SLOTS = 3
X_TILES = 2
PRE_TURNS = NT + 1
V_TURN = 6

STAGED_UNITS = (K_UNIT, Q_UNIT + 1)
V_TURN_STEPS = (1, 5)
CTX_EARLY = 6
SWAP_FROM = 0
C_TAKE = 1
ROWS_BLOCK = 2
ACT_NORM = 4
SPLIT_UNITS = {2: (0, 1), 3: (2, 3), 4: (4, 5)}
SPLIT_WO = {4: 0, 5: 1, 6: 2, 7: 3}


def gap_job(ls, gap, final=False):
    gl, i = divmod(ls, NT)
    k, part = {(0, "A"): (0, 0), (0, "B"): (0, 1), (0, "C"): (1, 0),
               (1, "A"): (1, 1), (1, "B"): (2, 0), (1, "C"): (2, 1)}[i % 2, gap]
    c, unit = divmod(3 * (i // 2) + k, UNITS)
    job = (gl + c, 1 - c, unit)
    return None if final and job[0] >= PAIR else (job, part)


def ended_job(ls, gap, final=False):
    found = gap_job(ls, gap, final)
    return found[0] if found and found[1] == 1 else None


def v_turn(ls, final):
    gl, i = divmod(ls, NT)
    if i == V_TURN_STEPS[0]:
        job = (gl, 1)
    elif i == V_TURN_STEPS[1] and not (final and gl == PAIR - 1):
        job = (gl + 1, 0)
    else:
        return None
    return turn_local(ls, i, final) + 1, half_slot(*job), job


def job_index(it, gl, c, unit):
    return it * (2 * UNITS * PAIR) + 2 * UNITS * gl + UNITS * c + unit


def rope_index(it, gl, c, unit):
    return it * (2 * (UNITS - 1) * PAIR) + 2 * (UNITS - 1) * gl + (UNITS - 1) * c + max(0, unit - 1)


def is_ahead(it, gl, c):
    return isinstance(it, int) and it == 0 and gl == 0 and c == 0


def staged(it, gl, c, unit):
    return unit in STAGED_UNITS and not is_ahead(it, gl, c)


def staged_index(it, gl, c, unit):
    half = len(STAGED_UNITS)
    before = sum(u in STAGED_UNITS for u in range(unit))
    return (it * PAIR + gl) * 2 * half + c * half + before - half


def v_index(it, gl, c):
    return it * (2 * PAIR) + 2 * gl + c


def turn_local(ls, t, final):
    gl, i = divmod(ls, NT)
    in_final = final and gl == PAIR - 1
    return gl * (BLOCKS + 2) + i * (i + 1) // 2 + t + (i > V_TURN_STEPS[0]) + (i > V_TURN_STEPS[1] and not in_final)


def x_turn(n):
    return n + (n >= V_TURN)


def block_local(ls, t):
    gl, i = divmod(ls, NT)
    return gl * BLOCKS + i * (i + 1) // 2 + t


def half_slot(gl, c):
    return 2 if c else gl % 2


def late_heads(ls):
    i = ls % NT
    return (1, R - 1) if i >= ACT_NORM and i % 2 == 1 else (R - 1,)


def late_index(it, ls):
    return it * sum(len(late_heads(j)) for j in range(STEPS)) + sum(len(late_heads(j)) for j in range(ls))


def early_index(it, ls):
    return (it * sum(R - len(late_heads(j)) for j in range(STEPS))
            + sum(R - len(late_heads(j)) for j in range(ls)))


def has_rest(ls):
    return ls % NT >= NT // 2


def rest_index(it, ls):
    gl, i = divmod(ls, NT)
    return it * (STEPS // 2) + gl * (NT // 2) + i - NT // 2


def score_base(i):
    return P if i == NT // 2 else 0


def score_parts(i):
    half = NT // 2
    if i < half:
        return [(0, max(2, i + 1))]
    cut = half - (i == half)
    return [(0, cut), (cut, i + 1)]


def key_blocks(t, gl, first, end):
    half = NT // 2
    blocks = t.rearrange("p s (b t) -> p (s b) t", t=P)
    places = [half_slot(gl, j // half) * half + j % half for j in range(first, end)]
    step = places[1] - places[0]
    return blocks[:, places[0]:places[-1] + 1:step, :]


def build(nc, x, wq, wk, wv, wo, biases, bo, cos_t, sin_t, aw, b_t, br, out):
    x_v = x.rearrange("a (n p) d -> p (a n) d", p=P)
    out_v = out.rearrange("a (n p) d -> p (a n) d", p=P)
    w_v = {K_UNIT: wk.rearrange("(k p) n -> p k n", p=P),
           V_UNIT: wv.rearrange("(k p) n -> p k n", p=P),
           Q_UNIT: wq.rearrange("(k p) n -> p k n", p=P)}
    aw_v = aw.rearrange("(k p) n -> p k n", p=P)

    with ExitStack() as ctx:
        def sb(name, shape, dt=F32):
            return ctx.enter_context(nc.sbuf_tensor(name, shape, dt))

        def ps(name, shape):
            return ctx.enter_context(nc.psum_tensor(name, shape, F32))

        def sem(name):
            return ctx.enter_context(nc.semaphore(name))

        xT_hi = sb("xT_hi", [P, KT, S], F32R)
        xT_lo = sb("xT_lo", [P, KT, S], F32R)
        kT_hi = sb("kT_hi", [P, 3, HALF], F32R)
        kT_lo = sb("kT_lo", [P, 3, HALF], F32R)
        v_hi = sb("v_hi", [P, 3, HALF // P, D], F32R)
        v_lo = sb("v_lo", [P, 3, HALF // P, D], F32R)
        qT_hi = sb("qT_hi", [P, R, S], F32R)
        qT_lo = sb("qT_lo", [P, R, S], F32R)
        w_hi = sb("w_hi", [P, UNITS, KT, D], F32R)
        w_lo = sb("w_lo", [P, UNITS, KT, D], F32R)
        wo_hi = sb("wo_hi", [P, 2, R, HID], F32R)
        wo_lo = sb("wo_lo", [P, 2, R, HID], F32R)
        w_stage = sb("w_stage", [P, 2, KT, D])
        wo_stage = sb("wo_stage", [P, 2, HID])
        cos_sb = sb("cos_sb", [P, S])
        sin_sb = sb("sin_sb", [P, S])
        acc = sb("acc", [P, NT, HID])
        probs = sb("probs", [P, R, S])
        pT_hi = sb("pT_hi", [P, PT_SLOTS, R * P], F32R)
        pT_lo = sb("pT_lo", [P, PT_SLOTS, R * P], F32R)
        rot = sb("rot", [P, 2, HALF])
        straight = sb("straight", [P, 2, HALF])
        vT = sb("vT", [P, HALF])
        ctx_hi = sb("ctx_hi", [P, R * P], F32R)
        ctx_lo = sb("ctx_lo", [P, R * P], F32R)
        bias_all = sb("bias_all", [P, G, UNITS])
        bias_now = sb("bias_now", [P, 2, UNITS])
        ident = sb("ident", [P, P])
        mask = sb("mask", [P, P])
        neg_max = sb("neg_max", [P, R])
        row_sum = sb("row_sum", [P, R])
        row_inv = sb("row_inv", [P, R])
        stats = sb("stats", [P, NT, 6])
        mean_var = sb("mean_var", [P, NT, 2])
        std = sb("std", [P, NT])
        rstd = sb("rstd", [P, NT])
        logits = sb("logits", [P, NT, E])
        br_sb = sb("br_sb", [P, E])
        gate_neg = sb("gate_neg", [P, NT])
        gate_sum = sb("gate_sum", [P, NT])
        gate_inv = sb("gate_inv", [P, NT])
        aw_sb = sb("aw_sb", [P, KT, ER + E])
        xn = probs[:, 0, :].rearrange("p (b d) -> p b d", b=2)
        xT_f = probs[:, 1, :].rearrange("p (b k t) -> p b k t", b=2, k=KT)
        low = probs[:, 2, :].rearrange("p (n e) -> p n e", e=ER)
        bo_sb = probs[:, 3, HID:2 * HID]
        lowT = w_stage.rearrange("p s n t -> p (s n) t")
        bt_sb = vT[:, :]
        score_ps = [ps("score0", [P, S]), ps("score1", [P, S])]
        turn_ps = [ps("turn0", [P, HID]), ps("turn1", [P, HID])]
        ctx_ps = ps("ctx", [P, HID])
        proj_ps = ps("proj", [P, HALF])

        ffn_ps = [score_ps[0][:, HID:S], score_ps[1][:, HID:S], ctx_ps[:, :]]

        x_loaded = [sem(f"x_loaded{c}") for c in range(NT // X_TILES)]
        aw_loaded, bias_loaded, br_loaded = sem("aw_loaded"), sem("bias_loaded"), sem("br_loaded")
        cos_loaded, sin_loaded = sem("cos_loaded"), sem("sin_loaded")
        bt_loaded, bo_loaded = sem("bt_loaded"), sem("bo_loaded")
        w_loaded = [sem("w_loaded0"), sem("w_loaded1")]
        wo_loaded = [sem("wo_loaded0"), sem("wo_loaded1")]
        out_stored = sem("out_stored")
        turned = sem("turned")
        scored = sem("scored")
        projected = sem("projected")
        block_summed = sem("block_summed")
        out_projected = sem("out_projected")
        gated_in = sem("gated_in")
        low_turned = sem("low_turned")
        ffn_out = sem("ffn_out")
        turn_hi = sem("turn_hi")
        exps = sem("exps")
        v_taken = sem("v_taken")
        straight_set = sem("straight_set")
        swapped = sem("swapped")
        ctx_hi_done = sem("ctx_hi_done")
        std_done = sem("std_done")
        xT_f_done = sem("xT_f_done")
        gate_exp = sem("gate_exp")
        lowT_done = sem("lowT_done")
        turn_lo = sem("turn_lo")
        masked = sem("masked")
        max_done = sem("max_done")
        inv_done = sem("inv_done")
        probs_done = sem("probs_done")
        late_probs_done = sem("late_probs_done")
        rest_done = sem("rest_done")
        cos_done = sem("cos_done")
        ctx_lo_done = sem("ctx_lo_done")
        acc_added = sem("acc_added")
        stats_done, mean_done, var_done, rstd_done = (sem(f"{x}_done") for x in ("stats", "mean", "var", "rstd"))
        w_hi_done, wo_hi_done = sem("w_hi_done"), sem("wo_hi_done")
        w_split, wo_split = sem("w_split"), sem("wo_split")
        xn_done = sem("xn_done")
        low_read = sem("low_read")
        gate_step = sem("gate_step")
        const_step = sem("const_step")
        consts_done = sem("consts_done")
        biases_set = sem("biases_set")
        bo_added = [sem("bo_added_first"), sem("bo_added_middle"), sem("bo_added_last")]
        sin_done, rope_summed, rope_hi = sem("sin_done"), sem("rope_summed"), sem("rope_hi")
        roped = sem("roped")

        block = ctx.enter_context(nc.Block())

        def probs_sem(ls, h):
            return late_probs_done if h in late_heads(ls) else probs_done

        def job_ps(it, gl, c, unit):
            return ctx_ps if is_ahead(it, gl, c) and unit % 2 == 1 else proj_ps

        def split_dst(gl, c, unit):
            if unit == K_UNIT:
                return kT_hi[:, half_slot(gl, c), :], kT_lo[:, half_slot(gl, c), :]
            h = unit - Q_UNIT
            return qT_hi[:, h, c * HALF:(c + 1) * HALF], qT_lo[:, h, c * HALF:(c + 1) * HALF]

        @block.sync
        def _(sp):
            def load_unit(g, u):
                view = w_v[min(u, Q_UNIT)]
                col = g * (R * D) + (u - Q_UNIT) * D if u >= Q_UNIT else g * D
                sp.dma_start(w_stage[:, u % 2], view[:, :, bass.ds(col, D)]).then_inc(w_loaded[u % 2], 16)

            def load_wo(g, h):
                sp.dma_start(wo_stage[:, h % 2, :], wo[bass.ds(g * (R * D) + h * D, D), :])\
                    .then_inc(wo_loaded[h % 2], 16)

            def load_x(c):
                tiles = slice(c * X_TILES, (c + 1) * X_TILES)
                sp.dma_start(acc[:, tiles, :], x_v[:, tiles, :]).then_inc(x_loaded[c], 16)

            load_x(0)
            load_x(1)
            load_unit(0, 0)
            load_unit(0, 1)
            load_x(2)
            load_x(3)
            load_wo(0, 0)
            load_wo(0, 1)
            for u in range(2, UNITS):
                sp.wait_ge(w_split, u - 1)
                load_unit(0, u)
            sp.wait_ge(turned, V_TURN + 1)
            sp.dma_start(bt_sb, b_t).then_inc(bt_loaded, 16)
            for h in range(2, R):
                sp.wait_ge(wo_split, h - 1)
                load_wo(0, h)
            sp.wait_ge(ffn_out, NT)

            def one_pass(it, final):
                for gl in range(PAIR):
                    if final and gl == PAIR - 1:
                        break
                    for u in range(UNITS):
                        sp.wait_ge(w_split, it * (UNITS * PAIR) + UNITS * (gl + 1) + u - 1)
                        load_unit(it * PAIR + gl + 1, u)
                    for h in range(R):
                        sp.wait_ge(wo_split, it * (R * PAIR) + R * (gl + 1) + h - 1)
                        load_wo(it * PAIR + gl + 1, h)

            with sp.Fori(0, PASSES - 1) as it:
                one_pass(it, False)
            one_pass(PASSES - 1, True)
            for i in range(NT):
                sp.wait_ge(acc_added, NT + (G - 1) * NT + i + 1)
                sp.dma_start(out_v[:, i, :], acc[:, i, :]).then_inc(out_stored, 16)
            sp.wait_ge(out_stored, 16 * NT)

        @block.gpsimd
        def _(pool):
            def split_unit(it, gl, u):
                n = it * (UNITS * PAIR) + UNITS * gl + u
                pool.wait_ge(w_hi_done, n + 1)
                pool.tensor_tensor(w_lo[:, u], w_stage[:, u % 2], w_hi[:, u].bitcast(F32),
                                   ALU.subtract).then_inc(w_split, 1)

            def split_wo(it, gl, h):
                n = it * (R * PAIR) + R * gl + h
                pool.wait_ge(wo_hi_done, n + 1)
                pool.tensor_tensor(wo_lo[:, gl % 2, h, :], wo_stage[:, h % 2, :],
                                   wo_hi[:, gl % 2, h, :].bitcast(F32), ALU.subtract).then_inc(wo_split, 1)

            def rope(it, gl, c, unit, cos=False, sin=True):
                n = rope_index(it, gl, c, unit)
                b = rope_index(0, gl, c, unit) % 2
                hi, lo = split_dst(gl, c, unit)
                if sin:
                    pool.wait_ge(swapped, (n + 1) * 2)
                if cos:
                    pool.wait_ge(cos_done, n)
                    pool.tensor_tensor(straight[:, b], straight[:, b], cos_sb[:, c * HALF:(c + 1) * HALF],
                                       ALU.mult).then_inc(cos_done, 1)
                if sin:
                    pool.tensor_tensor(rot[:, b], rot[:, b], sin_sb[:, c * HALF:(c + 1) * HALF],
                                       ALU.mult).then_inc(sin_done, 1)
                pool.wait_ge(sin_done, n + 1)
                pool.wait_ge(cos_done, n + 1)
                pool.tensor_tensor(hi, straight[:, b], rot[:, b], ALU.add).then_inc(rope_hi, 1)
                pool.wait_ge(rope_hi, n + 1)
                pool.tensor_tensor(straight[:, b], straight[:, b], rot[:, b], ALU.add).then_inc(rope_summed, 1)
                pool.wait_ge(rope_summed, n + 1)
                pool.tensor_tensor(lo, straight[:, b], hi.bitcast(F32), ALU.subtract).then_inc(roped, 1)

            def set_biases(g, slot):
                pool.tensor_copy(bias_now[:, slot:slot + 1, :], bias_all[:, bass.ds(g, 1), :]).then_inc(biases_set, 1)

            pool.memset(ident[:], 0.0).then_inc(const_step, 1)
            pool.memset(mask[:], 0.0).then_inc(const_step, 1)
            pool.wait_ge(const_step, 2)
            pool.affine_select(out=ident[:], in_=ident[:], compare_op=ALU.not_equal, fill=1.0, base=0,
                               pattern=[[-1, P]], channel_multiplier=1).then_inc(consts_done, 1)
            pool.affine_select(out=mask[:], in_=mask[:], compare_op=ALU.is_ge, fill=MASKED, base=0,
                               pattern=[[-1, P]], channel_multiplier=1).then_inc(consts_done, 1)
            pool.wait_ge(bias_loaded, 16)
            set_biases(0, 0)
            pool.wait_ge(bo_loaded, 16)

            def add_bo(n):
                pool.wait_ge(xn_done, n + 1)
                pool.tensor_tensor(acc[:, n, :], acc[:, n, :], bo_sb, ALU.add).then_inc(bo_added[n // 3], 1)

            add_bo(0)
            split_unit(0, 0, 2)
            add_bo(1)
            pool.wait_ge(cos_loaded, 16)
            pool.wait_ge(sin_loaded, 16)
            rope(0, 0, 0, K_UNIT, sin=False)
            split_unit(0, 0, 3)
            split_unit(0, 0, 4)
            add_bo(2)
            split_unit(0, 0, 5)
            rope(0, 0, 0, Q_UNIT, sin=False)
            rope(0, 0, 0, Q_UNIT + 1, sin=False)
            rope(0, 0, 0, Q_UNIT + 2, sin=False)
            rope(0, 0, 0, Q_UNIT + 3, sin=False)
            add_bo(6)
            add_bo(7)
            rope(0, *ended_job(0, "B"), cos=True)

            def one_pass(it, final):
                for ls in range(STEPS):
                    gl, i = divmod(ls, NT)
                    in_final = final and gl == PAIR - 1
                    job = ended_job(ls, "C", final)
                    if job and job[2] != V_UNIT:
                        rope(it, *job)
                    if not in_final:
                        for u in SPLIT_UNITS.get(i, ()):
                            split_unit(it, gl + 1, u)
                        if i == 1:
                            set_biases(it * PAIR + gl + 1, (gl + 1) % 2)
                        if i in SPLIT_WO:
                            split_wo(it, gl + 1, SPLIT_WO[i])
                    if final and ls == STEPS - 1:
                        break
                    for gap in "AB":
                        job = ended_job(ls + 1, gap, final)
                        if job and job[2] != V_UNIT:
                            rope(it, *job, cos=(gap == "B"))

            with pool.Fori(0, PASSES - 1) as it:
                one_pass(it, False)
            one_pass(PASSES - 1, True)

        @block.scalar
        def _(act):
            def take_job(it, gl, c, unit, parts=(0, 1)):
                if 0 in parts:
                    act.wait_ge(projected, job_index(it, gl, c, unit) + 1)
                bias = bias_now[:, gl % 2, unit:unit + 1]
                src = job_ps(it, gl, c, unit)
                if unit == V_UNIT:
                    act.activation(vT[:, :], src[:, :], ACT.Identity, bias=bias).then_inc(v_taken, 1)
                    return
                n = rope_index(it, gl, c, unit)
                b = rope_index(0, gl, c, unit) % 2
                if 0 in parts and not (isinstance(n, int) and n < 2):
                    act.wait_ge(roped, n - 1)
                if staged(it, gl, c, unit):
                    act.activation(straight[:, b, :], src[:, :], ACT.Identity, bias=bias).then_inc(straight_set, 1)
                    return
                m = D // 2
                for part in parts:
                    to, frm = (slice(0, m), slice(m, D)) if part == 0 else (slice(m, D), slice(0, m))
                    act.activation(rot[to, b, :], src[frm, :], ACT.Identity, bias=bias[frm]).then_inc(swapped, 1)

            def swap_staged(it, gl, c, unit, part):
                if part == 0:
                    act.wait_ge(straight_set, staged_index(it, gl, c, unit) + 1)
                b = rope_index(0, gl, c, unit) % 2
                m = D // 2
                to, frm = (slice(0, m), slice(m, D)) if part == 0 else (slice(m, D), slice(0, m))
                act.activation(rot[to, b, :], straight[frm, b, :], ACT.Copy).then_inc(swapped, 1)

            def exp_head(it, ls, h):
                n = it * (STEPS * R) + ls * R + h
                w = (ls % NT + 1) * P
                act.wait_ge(max_done, n + 1)
                b = score_base(ls % NT)
                act.activation(probs[:, h, 0:w], score_ps[h % 2][:, b:b + w], ACT.Exp, bias=neg_max[:, h:h + 1],
                               accum_out=row_sum[:, h:h + 1]).then_inc(exps, 1)

            def v_turn_hi(it, u, slot):
                act.wait_ge(turned, it * (PAIR * (BLOCKS + 2)) + PRE_TURNS + u + 1)
                act.activation(v_hi[:, slot].rearrange("p b d -> p (b d)"), turn_ps[(PRE_TURNS + u) % 2][:, :],
                               ACT.Copy).then_inc(turn_hi, 1)

            def normalise(it, ls, h):
                n = it * (STEPS * R) + ls * R + h
                w = (ls % NT + 1) * P
                act.wait_ge(inv_done, n + 1)
                act.activation(probs[:, h, 0:w], probs[:, h, 0:w], ACT.Copy,
                               scale=row_inv[:, h:h + 1]).then_inc(probs_sem(ls, h), 1)

            act.dma_start(aw_sb[:], aw_v).then_inc(aw_loaded, 16)

            def take_std(c):
                act.wait_ge(var_done, c + 1)
                tiles = slice(c * X_TILES, (c + 1) * X_TILES)
                act.activation(std[:, tiles], std[:, tiles], ACT.Sqrt).then_inc(std_done, 1)

            def take_x(n):
                u = x_turn(n)
                act.wait_ge(turned, u + 1)
                if n >= 2:
                    act.wait_ge(gated_in, n - 1)
                src = turn_ps[u % 2][:, :].rearrange("p (k t) -> p k t", k=KT)
                act.activation(xT_f[:, n % 2], src, ACT.Copy).then_inc(xT_f_done, 1)
                act.activation(xT_hi[:, :, n * P:(n + 1) * P], src, ACT.Copy).then_inc(turn_hi, 1)

            take_std(0)
            act.dma_start(bias_all[:], biases).then_inc(bias_loaded, 16)
            act.dma_start(br_sb[:], br.partition_broadcast(P)).then_inc(br_loaded, 16)
            act.dma_start(cos_sb[:], cos_t).then_inc(cos_loaded, 16)
            act.dma_start(sin_sb[:], sin_t).then_inc(sin_loaded, 16)
            act.dma_start(bo_sb, bo.partition_broadcast(P)).then_inc(bo_loaded, 16)
            take_x(0)
            take_std(1)
            take_x(1)
            take_x(2)
            take_x(3)
            take_std(2)
            act.wait_ge(biases_set, 1)
            take_job(0, 0, 0, K_UNIT)
            take_x(4)
            take_job(0, 0, 0, V_UNIT)
            take_std(3)
            take_x(5)
            take_job(0, 0, 0, Q_UNIT)
            act.wait_ge(turned, V_TURN + 1)
            act.activation(v_hi[:, 0].rearrange("p b d -> p (b d)"), turn_ps[V_TURN % 2][:, :],
                           ACT.Copy).then_inc(turn_hi, 1)
            take_x(6)
            take_job(0, 0, 0, Q_UNIT + 1)
            take_x(7)
            take_job(0, 0, 0, Q_UNIT + 2)
            act.wait_ge(gate_step, 3)
            act.activation(logits[:], logits[:], ACT.Exp).then_inc(gate_exp, 1)
            take_job(0, 0, 0, Q_UNIT + 3)
            for b in range(2):
                act.wait_ge(low_turned, b + 1)
                act.activation(lowT[:, b * 4:(b + 1) * 4, :].rearrange("p n t -> p (n t)"), score_ps[b][:, HID:S],
                               ACT.Copy).then_inc(lowT_done, 1)
            for h in range(R):
                exp_head(0, 0, h)
            take_job(0, *ended_job(0, "B"))
            for part in range(2):
                swap_staged(0, *ended_job(0, "B"), part)

            def one_pass(it, final):
                for ls in range(STEPS):
                    gl, i = divmod(ls, NT)
                    in_final = final and gl == PAIR - 1
                    job = ended_job(ls, "C", final)
                    late_swap = ended_job(ls, "B", final) if i > 0 else None
                    for t in range(i + 1):
                        u, p = turn_local(ls, t, final), block_local(ls, t)
                        act.wait_ge(turned, it * (PAIR * (BLOCKS + 2)) + PRE_TURNS + u + 1)
                        act.wait_ge(block_summed, it * (PAIR * BLOCKS) + p + 1)
                        act.activation(pT_hi[:, p % PT_SLOTS, :], turn_ps[(PRE_TURNS + u) % 2][:, :],
                                       ACT.Copy).then_inc(turn_hi, 1)
                        for part in range(2 if late_swap else 0):
                            if t == min(i, SWAP_FROM + part):
                                swap_staged(it, *late_swap, part)
                        if job and t == min(i, C_TAKE):
                            take_job(it, *job, parts=(0,))
                        if job and t == min(i, C_TAKE + 1) and job[2] != V_UNIT:
                            take_job(it, *job, parts=(1,))
                    v = v_turn(ls, final)
                    if v:
                        v_turn_hi(it, v[0], v[1])
                    act.wait_ge(block_summed, it * (PAIR * BLOCKS) + block_local(ls, i) + 1 + PT_SLOTS)
                    act.activation(ctx_hi[:], ctx_ps[:, :], ACT.Copy).then_inc(ctx_hi_done, 1)
                    if final and ls == STEPS - 1:
                        break
                    act_norm = (ls + 1) % NT >= ACT_NORM
                    late = 1 in late_heads(ls + 1)
                    a_job, b_job = ended_job(ls + 1, "A", final), ended_job(ls + 1, "B", final)
                    exp_head(it, ls + 1, 0)
                    exp_head(it, ls + 1, 1)
                    if act_norm:
                        normalise(it, ls + 1, 0)
                    if a_job:
                        take_job(it, *a_job)
                    exp_head(it, ls + 1, 2)
                    if act_norm and not late:
                        normalise(it, ls + 1, 1)
                    exp_head(it, ls + 1, 3)
                    if act_norm and late:
                        normalise(it, ls + 1, 1)
                    if b_job:
                        if b_job[2] == K_UNIT:
                            act.wait_ge(biases_set, it * PAIR + b_job[0] + 1)
                        take_job(it, *b_job)
                        if (ls + 1) % NT == 0:
                            for part in range(2):
                                swap_staged(it, *b_job, part)

            with act.Fori(0, PASSES - 1) as it:
                one_pass(it, False)
            one_pass(PASSES - 1, True)

        @block.vector
        def _(dve):
            def lo_part(out_lo, src_ps, hi):
                return dve.tensor_tensor(out_lo, src_ps, hi.bitcast(F32), ALU.subtract)

            def times_cos(it, gl, c, unit):
                n = rope_index(it, gl, c, unit)
                b = rope_index(0, gl, c, unit) % 2
                dve.wait_ge(swapped, (n + 1) * 2)
                if not (isinstance(n, int) and n < 2):
                    dve.wait_ge(roped, n - 1)
                    dve.wait_ge(cos_done, n)
                dve.scalar_tensor_tensor(straight[:, b], job_ps(it, gl, c, unit)[:, :], bias_now[:, gl % 2, unit:unit + 1],
                                         cos_sb[:, c * HALF:(c + 1) * HALF], ALU.add, ALU.mult)\
                    .then_inc(cos_done, 1)

            def row_max(it, ls, h):
                n = it * (STEPS * R) + ls * R + h
                w = (ls % NT + 1) * P
                dve.wait_ge(scored, n + 1)
                o = score_ps[h % 2][:, score_base(ls % NT):score_base(ls % NT) + w]
                dve.tensor_tensor(o[:, w - P:w], o[:, w - P:w], mask[:], ALU.add).then_inc(masked, 1)
                dve.wait_ge(masked, n + 1)
                dve.tensor_reduce(neg_max[:, h:h + 1], o, AX.X, ALU.max, negate=True).then_inc(max_done, 1)

            def invert(it, ls, h):
                n = it * (STEPS * R) + ls * R + h
                dve.wait_ge(exps, n + 1)
                dve.reciprocal(row_inv[:, h:h + 1], row_sum[:, h:h + 1]).then_inc(inv_done, 1)

            def normalise(it, ls, h):
                n = it * (STEPS * R) + ls * R + h
                w = (ls % NT + 1) * P
                invert(it, ls, h)
                if ls % NT >= ACT_NORM and h < 2:
                    return
                dve.wait_ge(inv_done, n + 1)
                m = 2 * P if h == R - 1 and has_rest(ls) else w
                dve.tensor_scalar(probs[:, h, 0:m], probs[:, h, 0:m], row_inv[:, h:h + 1], None, ALU.mult)\
                    .then_inc(probs_sem(ls, h), 1)
                if m < w:
                    dve.tensor_scalar(probs[:, h, m:w], probs[:, h, m:w], row_inv[:, h:h + 1], None, ALU.mult)\
                        .then_inc(rest_done, 1)

            def score_part(it, ls, final):
                row_max(it, ls, 0)
                if ls % NT < CTX_EARLY:
                    row_max(it, ls, 1)
                dve.wait_ge(ctx_hi_done, it * STEPS + ls)
                lo_part(ctx_lo[:], ctx_ps[:, :], ctx_hi[:]).then_inc(ctx_lo_done, 1)
                if ls % NT >= CTX_EARLY:
                    row_max(it, ls, 1)
                normalise(it, ls, 0)
                act_norm = ls % NT >= ACT_NORM
                if not act_norm:
                    normalise(it, ls, 1)
                row_max(it, ls, 2)
                if act_norm:
                    normalise(it, ls, 1)
                a_job = ended_job(ls, "A", final)
                if act_norm:
                    row_max(it, ls, 3)
                if a_job and a_job[2] != V_UNIT:
                    times_cos(it, *a_job)
                if not act_norm:
                    row_max(it, ls, 3)
                normalise(it, ls, 2)
                normalise(it, ls, 3)

            def unit_hi(it, gl, u):
                dve.wait_ge(w_loaded[u % 2], (it * (UNITS * PAIR // 2) + UNITS // 2 * gl + u // 2 + 1) * 16)
                dve.tensor_copy(w_hi[:, u], w_stage[:, u % 2]).then_inc(w_hi_done, 1)

            def rows_hi(it, gl, h):
                dve.wait_ge(wo_loaded[h % 2], (it * (R * PAIR // 2) + R // 2 * gl + h // 2 + 1) * 16)
                dve.tensor_copy(wo_hi[:, gl % 2, h, :], wo_stage[:, h % 2, :]).then_inc(wo_hi_done, 1)

            def stats_of(c):
                tiles = range(c * X_TILES, (c + 1) * X_TILES)
                dve.wait_ge(x_loaded[c], 16)
                for n in tiles:
                    dve.bn_stats(stats[:, n, :], acc[:, n, :]).then_inc(stats_done, 1)
                for n in tiles:
                    dve.wait_ge(stats_done, n + 1)
                    dve.bn_aggr(mean_var[:, n, :], stats[:, n, :]).then_inc(mean_done, 1)
                dve.wait_ge(mean_done, tiles.stop)
                cols = slice(tiles.start, tiles.stop)
                dve.tensor_scalar(std[:, cols], mean_var[:, cols, 1], EPS, None, ALU.add).then_inc(var_done, 1)

            def invert_std(c):
                cols = slice(c * X_TILES, (c + 1) * X_TILES)
                dve.wait_ge(std_done, c + 1)
                dve.reciprocal(rstd[:, cols], std[:, cols]).then_inc(rstd_done, 1)
                dve.wait_ge(rstd_done, c + 1)

            def normal_x(n):
                if n >= 2:
                    dve.wait_ge(turned, x_turn(n - 2) + 1)
                dve.tensor_scalar(xn[:, n % 2], acc[:, n, :], mean_var[:, n, 0:1], rstd[:, n:n + 1],
                                  ALU.subtract, ALU.mult).then_inc(xn_done, 1)

            def x_lo(n):
                u = x_turn(n)
                dve.wait_ge(turn_hi, u + 1)
                lo_part(xT_lo[:, :, n * P:(n + 1) * P],
                        turn_ps[u % 2][:, :].rearrange("p (k t) -> p k t", k=KT),
                        xT_hi[:, :, n * P:(n + 1) * P]).then_inc(turn_lo, 1)

            def take_low(n):
                dve.wait_ge(gated_in, n + 1)
                dve.tensor_copy(logits[:, n, :], score_ps[n % 2][:, ER:ER + E]).then_inc(low_read, 1)
                dve.tensor_copy(low[:, n, :], score_ps[n % 2][:, 0:ER]).then_inc(low_read, 1)

            def first_unit(u):
                unit_hi(0, 0, u)
                dve.wait_ge(w_hi_done, u + 1)
                dve.tensor_tensor(w_lo[:, u], w_stage[:, u % 2], w_hi[:, u].bitcast(F32),
                                  ALU.subtract).then_inc(w_split, 1)

            def first_rows(h):
                rows_hi(0, 0, h)
                dve.wait_ge(wo_hi_done, h + 1)
                dve.tensor_tensor(wo_lo[:, 0, h, :], wo_stage[:, h % 2, :], wo_hi[:, 0, h, :].bitcast(F32),
                                  ALU.subtract).then_inc(wo_split, 1)

            def first_rope(unit):
                times_cos(0, 0, 0, unit)
                b = rope_index(0, 0, 0, unit) % 2
                dve.tensor_tensor(rot[:, b], rot[:, b], sin_sb[:, 0:HALF], ALU.mult).then_inc(sin_done, 1)

            stats_of(0)
            invert_std(0)
            normal_x(0)
            normal_x(1)
            stats_of(1)
            first_unit(0)
            invert_std(1)
            normal_x(2)
            x_lo(0)
            normal_x(3)
            x_lo(1)
            take_low(0)
            x_lo(2)
            take_low(1)
            x_lo(3)
            stats_of(2)
            first_unit(1)
            invert_std(2)
            normal_x(4)
            normal_x(5)
            unit_hi(0, 0, 2)
            dve.wait_ge(cos_loaded, 16)
            dve.wait_ge(sin_loaded, 16)
            dve.wait_ge(biases_set, 1)
            first_rope(K_UNIT)
            take_low(2)
            stats_of(3)
            x_lo(4)
            unit_hi(0, 0, 3)
            invert_std(3)
            normal_x(6)
            take_low(3)
            x_lo(5)
            unit_hi(0, 0, 4)
            first_rows(0)
            first_rope(Q_UNIT)
            dve.wait_ge(turn_hi, V_TURN + 1)
            lo_part(v_lo[:, 0].rearrange("p b d -> p (b d)"), turn_ps[V_TURN % 2][:, :],
                    v_hi[:, 0].rearrange("p b d -> p (b d)")).then_inc(turn_lo, 1)
            unit_hi(0, 0, 5)
            normal_x(7)
            take_low(4)
            x_lo(6)
            first_rope(Q_UNIT + 1)
            take_low(5)
            x_lo(7)
            take_low(6)
            dve.wait_ge(bo_loaded, 16)
            for n in (3, 4, 5):
                dve.wait_ge(xn_done, n + 1)
                dve.tensor_tensor(acc[:, n, :], acc[:, n, :], bo_sb, ALU.add).then_inc(bo_added[1], 1)
            take_low(7)
            first_rope(Q_UNIT + 2)
            dve.wait_ge(low_read, 2 * NT)
            dve.wait_ge(br_loaded, 16)
            dve.tensor_tensor(logits[:], logits[:], br_sb[:, None, :].to_broadcast([P, NT, E]), ALU.add)\
                .then_inc(gate_step, 1)
            dve.wait_ge(gate_step, 1)
            dve.tensor_reduce(gate_neg[:], logits[:], AX.X, ALU.max).then_inc(gate_step, 1)
            dve.wait_ge(gate_step, 2)
            dve.tensor_tensor(logits[:], logits[:], gate_neg[:, :, None].to_broadcast([P, NT, E]), ALU.subtract)\
                .then_inc(gate_step, 1)
            dve.wait_ge(gate_exp, 1)
            dve.tensor_reduce(gate_sum[:], logits[:], AX.X, ALU.add).then_inc(gate_step, 1)
            dve.wait_ge(gate_step, 4)
            dve.reciprocal(gate_inv[:], gate_sum[:]).then_inc(gate_step, 1)
            dve.wait_ge(gate_step, 5)
            dve.tensor_scalar(gate_inv[:], gate_inv[:], FFN_SCALE, None, ALU.mult).then_inc(gate_step, 1)
            dve.wait_ge(gate_step, 6)
            dve.tensor_tensor(logits[:], logits[:], gate_inv[:, :, None].to_broadcast([P, NT, E]), ALU.mult)\
                .then_inc(gate_step, 1)
            dve.wait_ge(gate_step, 7)
            low_e = low.rearrange("p n (e r) -> p (n e) r", e=E)
            dve.tensor_tensor(low_e, low_e,
                              logits[:].rearrange("p n e -> p (n e)")[:, :, None].to_broadcast([P, NT * E, RANK]),
                              ALU.mult).then_inc(gate_step, 1)

            def add_ffn(n):
                dve.wait_ge(ffn_out, n + 1)
                dve.wait_ge(bo_added[n // 3], n % 3 + 1)
                dve.tensor_tensor(acc[:, n, :], ffn_ps[n % 3], acc[:, n, :], ALU.add).then_inc(acc_added, 1)

            first_rope(Q_UNIT + 3)
            dve.wait_ge(consts_done, 2)
            row_max(0, 0, 0)
            row_max(0, 0, 1)
            normalise(0, 0, 0)
            normalise(0, 0, 1)
            for n in range(3):
                add_ffn(n)
            row_max(0, 0, 2)
            add_ffn(3)
            first_rows(1)
            add_ffn(4)
            row_max(0, 0, 3)
            normalise(0, 0, 2)
            add_ffn(5)
            normalise(0, 0, 3)
            add_ffn(6)
            add_ffn(7)
            first_rows(2)
            first_rows(3)

            def v_turn_lo(it, u, slot):
                dve.wait_ge(turn_hi, it * (PAIR * (BLOCKS + 2)) + PRE_TURNS + u + 1)
                lo_part(v_lo[:, slot].rearrange("p b d -> p (b d)"), turn_ps[(PRE_TURNS + u) % 2][:, :],
                        v_hi[:, slot].rearrange("p b d -> p (b d)")).then_inc(turn_lo, 1)

            def add_output(it, ls):
                i = ls % NT
                dve.wait_ge(out_projected, it * STEPS + ls + 1)
                dve.tensor_tensor(acc[:, i, :], ctx_ps[:, :], acc[:, i, :], ALU.add).then_inc(acc_added, 1)

            def next_weights(it, ls, t):
                gl, i = divmod(ls, NT)
                for n, u in enumerate(SPLIT_UNITS.get(i, ())):
                    if t == (1, i)[n]:
                        dve.wait_ge(projected, job_index(it, gl, 1, u) + 1)
                        unit_hi(it, gl + 1, u)
                if i in SPLIT_WO and t == ROWS_BLOCK:
                    dve.wait_ge(out_projected, it * STEPS + ls)
                    rows_hi(it, gl + 1, SPLIT_WO[i])

            def one_pass(it, final):
                for ls in range(STEPS):
                    gl, i = divmod(ls, NT)
                    in_final = final and gl == PAIR - 1
                    job = ended_job(ls, "C", final)
                    for t in range(i + 1):
                        u, p = turn_local(ls, t, final), block_local(ls, t)
                        dve.wait_ge(turn_hi, it * (PAIR * (BLOCKS + 2)) + PRE_TURNS + u + 1)
                        lo_part(pT_lo[:, p % PT_SLOTS, :], turn_ps[(PRE_TURNS + u) % 2][:, :],
                                pT_hi[:, p % PT_SLOTS, :]).then_inc(turn_lo, 1)
                        if not in_final:
                            next_weights(it, ls, t)
                        if job and t == min(i, C_TAKE + 2) and job[2] != V_UNIT:
                            times_cos(it, *job)
                    v = v_turn(ls, final)
                    if v:
                        v_turn_lo(it, v[0], v[1])
                    if final and ls == STEPS - 1:
                        dve.wait_ge(ctx_hi_done, it * STEPS + ls + 1)
                        lo_part(ctx_lo[:], ctx_ps[:, :], ctx_hi[:]).then_inc(ctx_lo_done, 1)
                    else:
                        score_part(it, ls + 1, final)
                    add_output(it, ls)

            with dve.Fori(0, PASSES - 1) as it:
                one_pass(it, False)
            one_pass(PASSES - 1, True)

        @block.tensor
        def _(pe):
            def output(gl, heads):
                for h in heads:
                    w_h, w_l = wo_hi[:, gl % 2, h, :], wo_lo[:, gl % 2, h, :]
                    c_h, c_l = ctx_hi[:, h * P:(h + 1) * P], ctx_lo[:, h * P:(h + 1) * P]
                    pe.matmul(ctx_ps[:, :], c_h, w_h, start=(h == 0), stop=False)
                    pe.matmul(ctx_ps[:, :], c_h, w_l, start=False, stop=False)
                    last = pe.matmul(ctx_ps[:, :], c_l, w_h, start=False, stop=(h == R - 1))
                return last

            def project(it, job, part):
                gl, c, unit = job
                if part == 0:
                    if is_ahead(it, gl, c):
                        if unit == V_UNIT + 2:
                            pe.wait_ge(v_taken, 1)
                        elif unit >= 2:
                            pe.wait_ge(cos_done, max(1, unit - 2))
                    elif isinstance(it, int) and it == 0 and gl == 0 and unit == 0:
                        pe.wait_ge(cos_done, UNITS - 2)
                    elif unit == V_UNIT + 1:
                        pe.wait_ge(v_taken, v_index(it, gl, c) + 1)
                    elif unit > 0 and staged(it, gl, c, unit - 1):
                        pe.wait_ge(straight_set, staged_index(it, gl, c, unit - 1) + 1)
                    else:
                        pe.wait_ge(cos_done, rope_index(it, gl, c, unit) + (unit == V_UNIT))
                    if c == 0:
                        pe.wait_ge(w_split, it * (UNITS * PAIR) + UNITS * gl + unit + 1)
                cols = slice(c * HALF, (c + 1) * HALF)
                o = job_ps(it, gl, c, unit)
                for k in (range(KT // 2) if part == 0 else range(KT // 2, KT)):
                    pe.matmul(o[:, :], w_hi[:, unit, k, :], xT_hi[:, k, cols], start=(k == 0), stop=False)
                    pe.matmul(o[:, :], w_hi[:, unit, k, :], xT_lo[:, k, cols], start=False, stop=False)
                    last = pe.matmul(o[:, :], w_lo[:, unit, k, :], xT_hi[:, k, cols],
                                     start=False, stop=(k == KT - 1))
                if part == 1:
                    last.then_inc(projected, 1)

            def fill(it, ls, gap, final=False):
                found = gap_job(ls, gap, final)
                if found:
                    project(it, *found)

            def score(it, ls, h):
                gl, i = divmod(ls, NT)
                n = it * (STEPS * R) + ls * R + h
                if not (isinstance(n, int) and n < 2):
                    pe.wait_ge(exps, n - 1)
                if i % (NT // 2) == 0:
                    pe.wait_ge(roped, rope_index(it, gl, i // (NT // 2), Q_UNIT + h) + 1)
                q_hi, q_lo = qT_hi[:, h, i * P:(i + 1) * P], qT_lo[:, h, i * P:(i + 1) * P]
                base = score_base(i)
                for first, last_block in score_parts(i):
                    m = (last_block - first) * P
                    o = score_ps[h % 2][:, base + first * P:base + first * P + m]
                    k_hi, k_lo = (key_blocks(t, gl, first, last_block) for t in (kT_hi, kT_lo))
                    pe.matmul(o, q_hi, k_hi, start=True, stop=False)
                    pe.matmul(o, q_hi, k_lo, start=False, stop=False)
                    last = pe.matmul(o, q_lo, k_hi, start=False, stop=True)
                last.then_inc(scored, 1)

            def turn_v(u):
                for b in range(HALF // P):
                    last = pe.transpose(turn_ps[u % 2][:, b * P:(b + 1) * P], vT[:, b * P:(b + 1) * P], ident[:])
                last.then_inc(turned, 1)

            pe.wait_ge(consts_done, 1)
            pe.wait_ge(aw_loaded, 16)

            def gate_in(n):
                pe.wait_ge(xT_f_done, n + 1)
                if n >= 2:
                    pe.wait_ge(low_read, 2 * (n - 1))
                for k in range(KT):
                    last = pe.matmul(score_ps[n % 2][:, 0:ER + E], xT_f[:, n % 2, k, :], aw_sb[:, k, :],
                                     start=(k == 0), stop=(k == KT - 1))
                last.then_inc(gated_in, 1)

            def turn_x(n):
                u = x_turn(n)
                pe.wait_ge(xn_done, n + 1)
                if u >= 2:
                    pe.wait_ge(turn_lo, u - 1)
                for k in range(KT):
                    last = pe.transpose(turn_ps[u % 2][:, k * P:(k + 1) * P], xn[:, n % 2, k * P:(k + 1) * P],
                                        ident[:])
                    if n == 0 and k < PT_SLOTS:
                        last.then_inc(block_summed, 1)
                last.then_inc(turned, 1)

            def first_job(unit):
                project(0, (0, 0, unit), 0)
                project(0, (0, 0, unit), 1)

            turn_x(0)
            turn_x(1)
            gate_in(0)
            turn_x(2)
            gate_in(1)
            turn_x(3)
            pe.wait_ge(turn_lo, 4)
            first_job(K_UNIT)
            gate_in(2)
            turn_x(4)
            first_job(V_UNIT)
            gate_in(3)
            turn_x(5)
            first_job(Q_UNIT)
            pe.wait_ge(v_taken, 1)
            pe.wait_ge(turn_lo, V_TURN - 1)
            turn_v(V_TURN)
            gate_in(4)
            turn_x(6)
            first_job(Q_UNIT + 1)
            gate_in(5)
            turn_x(7)
            gate_in(6)
            first_job(Q_UNIT + 2)
            gate_in(7)
            first_job(Q_UNIT + 3)
            pe.wait_ge(low_read, 2 * NT)
            score(0, 0, 0)
            score(0, 0, 1)
            pe.wait_ge(turn_lo, PRE_TURNS)
            fill(0, 0, "A")
            pe.wait_ge(gate_step, 8)
            for n in range(NT):
                last = pe.transpose(score_ps[n // 4][:, HID + n % 4 * P:HID + (n % 4 + 1) * P], low[:, n, :], ident[:])
                if n % 4 == 3:
                    last.then_inc(low_turned, 1)

            def ffn(n):
                if n == 0:
                    pe.wait_ge(bt_loaded, 16)
                    pe.wait_ge(lowT_done, 1)
                if n == 1:
                    pe.wait_ge(lowT_done, 2)
                if n == 2:
                    pe.wait_ge(cos_done, UNITS - 1)
                if n >= 3:
                    pe.wait_ge(acc_added, n - 2)
                pe.matmul(ffn_ps[n % 3], lowT[:, n, :], bt_sb, start=True, stop=True).then_inc(ffn_out, 1)

            for n in range(4):
                ffn(n)
            score(0, 0, 2)
            ffn(4)
            score(0, 0, 3)
            for n in range(5, NT):
                ffn(n)
            fill(0, 0, "B")

            def one_pass(it, final):
                for ls in range(STEPS):
                    gl, i = divmod(ls, NT)
                    in_final = final and gl == PAIR - 1
                    turns = it * (PAIR * (BLOCKS + 2)) + PRE_TURNS

                    def turn(t, heads=range(R)):
                        u = turn_local(ls, t, final)
                        if heads[0] == 0:
                            pe.wait_ge(turn_lo, turns + u - 1)
                        if t == 2 and has_rest(ls):
                            pe.wait_ge(rest_done, rest_index(it, ls) + 1)
                        for h in heads:
                            last = pe.transpose(turn_ps[(PRE_TURNS + u) % 2][:, h * P:(h + 1) * P],
                                                probs[:, h, t * P:(t + 1) * P], ident[:])
                        if heads[-1] == R - 1:
                            last.then_inc(turned, 1)

                    pe.wait_ge(probs_done, early_index(it, ls + 1))
                    early = [h for h in range(R) if h not in late_heads(ls)]
                    for t in range(min(i + 1, 2)):
                        turn(t, early)
                    pe.wait_ge(late_probs_done, late_index(it, ls + 1))
                    for t in range(min(i + 1, 2)):
                        turn(t, late_heads(ls))
                    fill(it, ls, "C", final)
                    last_step = final and ls == STEPS - 1
                    v = v_turn(ls, final)
                    for t in range(i + 1):
                        if t == i and v:
                            pe.wait_ge(v_taken, v_index(it, *v[2]) + 1)
                            pe.wait_ge(turn_lo, turns + v[0] - 1)
                            turn_v(PRE_TURNS + v[0])
                        if t == i and not last_step:
                            score(it, ls + 1, 0)
                        if t + 2 <= i:
                            turn(t + 2)
                        u, p = turn_local(ls, t, final), block_local(ls, t)
                        if t == 0:
                            pe.wait_ge(acc_added, it * STEPS + NT + ls)
                        pe.wait_ge(turn_lo, turns + u + 1)
                        slot, b = half_slot(gl, t // (NT // 2)), t % (NT // 2)
                        pe.matmul(ctx_ps[:, :], v_hi[:, slot, b, :], pT_hi[:, p % PT_SLOTS, :],
                                  start=(t == 0), stop=False)
                        pe.matmul(ctx_ps[:, :], v_lo[:, slot, b, :], pT_hi[:, p % PT_SLOTS, :],
                                  start=False, stop=False)
                        last = pe.matmul(ctx_ps[:, :], v_hi[:, slot, b, :], pT_lo[:, p % PT_SLOTS, :],
                                         start=False, stop=(t == i))
                        last.then_inc(block_summed, 1)
                    if not last_step:
                        score(it, ls + 1, 1)
                        fill(it, ls + 1, "A", final)
                        score(it, ls + 1, 2)
                    pe.wait_ge(ctx_lo_done, it * STEPS + ls + 1)
                    if i == 0:
                        pe.wait_ge(wo_split, it * (R * PAIR) + R * gl + R)
                    ahead = 2 if (i + 1) % NT == NT // 2 else 1
                    output(gl, range(ahead))
                    if not last_step:
                        score(it, ls + 1, 3)
                        if i % 2 == 1:
                            fill(it, ls + 1, "B", final)
                    output(gl, range(ahead, R)).then_inc(out_projected, 1)
                    if i % 2 == 0:
                        fill(it, ls + 1, "B", final)

            with pe.Fori(0, PASSES - 1) as it:
                one_pass(it, False)
            one_pass(PASSES - 1, True)


def rope_tables():
    half = D // 2
    inv = (1.0 / np.float32(10000.0) ** (np.arange(half, dtype=np.float32) / np.float32(half))).astype(np.float32)
    ang = (np.arange(S, dtype=np.float32)[None, :] * inv[:, None]).astype(np.float32).astype(np.float64)
    cos, sin = ((ROOT_SCALE * f(ang)).astype(np.float32) for f in (np.cos, np.sin))
    return np.concatenate([cos, cos]), np.concatenate([-sin, sin])


def kernel(**inputs):
    import numpy as _np
    import concourse.bacc as _bacc
    from concourse import mybir as _mybir
    from concourse.bass_utils import run_bass_kernel_spmd as _run

    nc = _bacc.Bacc("TRN2", target_bir_lowering=False, num_devices=1, dynamic_dma_scratch_size=1024)
    a = {k[3:]: _np.asarray(v) for k, v in inputs.items()}
    cos_t, sin_t = rope_tables()
    per_group = [a["attn_bk"].reshape(G, 1, D), a["attn_bv"].reshape(G, 1, D), a["attn_bq"].reshape(G, R, D)]
    arrays = {
        "x": a["attn_hidden_states"], "wq": a["attn_Wq"], "wk": a["attn_Wk"], "wv": a["attn_Wv"],
        "wo": a["attn_Wo"],
        "biases": _np.concatenate(per_group, axis=1).transpose(2, 0, 1),
        "bo": a["attn_bo"], "cos_t": cos_t, "sin_t": sin_t,
        "aw": _np.concatenate([a["ffn_A"].reshape(ER, HID), a["ffn_Wr"]]).transpose(1, 0),
        "b_t": a["ffn_B"].transpose(0, 2, 1).reshape(ER, HID),
        "br": a["ffn_br"],
    }
    arrays = {k: _np.ascontiguousarray(v) for k, v in arrays.items()}
    args = [nc.dram_tensor(k, v.shape, _mybir.dt.from_np(v.dtype), kind="ExternalInput").ap()
            for k, v in arrays.items()]
    out = nc.dram_tensor("out", (1, S, HID), _mybir.dt.float32, kind="ExternalOutput").ap()
    build(nc, *args, out)
    r = _run(nc, [arrays], core_ids=[0])
    return r.results[0]["out"]
```
